# Optimizing a Trainium2 kernel written in Bass

```python
import numpy as np
import jax
import jax.numpy as jnp

def _softmax(x, axis=-1):
    return jax.nn.softmax(x, axis=axis)

def _gelu(x):
    return jax.nn.gelu(x, approximate=True)

def _silu(x):
    return jax.nn.silu(x)

def _sigmoid(x):
    return jax.nn.sigmoid(x)

def _layernorm(x, axis=-1, eps=1e-05):
    m = jnp.mean(x, axis=axis, keepdims=True)
    v = jnp.var(x, axis=axis, keepdims=True)
    return (x - m) / jnp.sqrt(v + eps)

def _scatter_add(tgt, idx, src, axis=0):
    return tgt.at[idx].add(src)

def _segment_sum(src, seg, n):
    return jax.ops.segment_sum(src, seg, n)
kernel_name = 'mk_adj_resnorm_d2_adj_r2_bcf7e0'

def setup_inputs(seed: int=0):
    np.random.seed(seed)
    _w = jnp.asarray

    def _rec_inputs():
        import jax
        import jax.numpy as jnp
        _gk = jax.random.key(seed)
        x = 7.22e-05 + 1 * jax.random.normal(jax.random.fold_in(_gk, 1), (32, 256, 256), jnp.float32)
        _a = jax.random.bernoulli(jax.random.fold_in(_gk, 2), 0.015625, (32, 256, 256))
        _a = jnp.logical_or(_a, jnp.swapaxes(_a, -1, -2))
        _a = jnp.logical_or(_a, jnp.eye(256, dtype=bool))
        _af = _a.astype(jnp.float32)
        _af = _af * jax.random.uniform(jax.random.fold_in(_gk, 3), (32, 256, 256), jnp.float32, 0.05, 1)
        adj = _af
        return (x, adj)
    x, adj = _rec_inputs()

    def _L0_gnn_setup():
        import jax, jax.numpy as jnp
        import numpy as np
        B, N, D = (8, 1024, 256)
        key = jax.random.key(seed)
        ks = jax.random.split(key, 8)
        scale = 0.5 / np.sqrt(D)
        x = jax.random.normal(ks[0], (B, N, D), dtype=jnp.float32)
        adj = jax.random.uniform(ks[1], (B, N, N), dtype=jnp.float32)
        Wq_w = jax.random.normal(ks[2], (D, D), dtype=jnp.float32) * scale
        Wk_w = jax.random.normal(ks[3], (D, D), dtype=jnp.float32) * scale
        Wv_w = jax.random.normal(ks[4], (D, D), dtype=jnp.float32) * scale
        Wq_b = jnp.zeros((D,), dtype=jnp.float32)
        Wk_b = jnp.zeros((D,), dtype=jnp.float32)
        Wv_b = jnp.zeros((D,), dtype=jnp.float32)
        return {'x': x, 'adj': adj, 'Wq_w': Wq_w, 'Wq_b': Wq_b, 'Wk_w': Wk_w, 'Wk_b': Wk_b, 'Wv_w': Wv_w, 'Wv_b': Wv_b}
    _L0_gnn_all = _L0_gnn_setup()
    _L0_gnn_in = {k: v for k, v in _L0_gnn_all.items() if k in ('Wq_w', 'Wq_b', 'Wk_w', 'Wk_b', 'Wv_w', 'Wv_b')}
    del _L0_gnn_all

    def _L1_gnn_setup():
        import jax, jax.numpy as jnp
        import numpy as np
        EMBED_DIM = 256
        NUM_HEADS = 8
        HEAD_DIM = EMBED_DIM // NUM_HEADS
        SCALE = HEAD_DIM ** (-0.5)
        B, S = (16, 512)
        key = jax.random.key(seed)
        ks = jax.random.split(key, 12)
        init = lambda k, shape: jax.random.normal(k, shape, dtype=jnp.float32) * EMBED_DIM ** (-0.5)
        return {'x': jax.random.normal(ks[0], (B, S, EMBED_DIM), dtype=jnp.float32), 'adj_matrix': jax.random.uniform(ks[1], (B, S, S), dtype=jnp.float32), 'bond_matrix': jax.random.uniform(ks[2], (B, S, S), dtype=jnp.float32), 'Wq': init(ks[3], (EMBED_DIM, EMBED_DIM)), 'bq': jnp.zeros((EMBED_DIM,), jnp.float32), 'Wk': init(ks[4], (EMBED_DIM, EMBED_DIM)), 'bk': jnp.zeros((EMBED_DIM,), jnp.float32), 'Wv': init(ks[5], (EMBED_DIM, EMBED_DIM)), 'bv': jnp.zeros((EMBED_DIM,), jnp.float32), 'Wo': init(ks[6], (EMBED_DIM, EMBED_DIM)), 'bo': jnp.zeros((EMBED_DIM,), jnp.float32), 'seq_len': S}
    _L1_gnn_all = _L1_gnn_setup()
    _L1_gnn_in = {k: v for k, v in _L1_gnn_all.items() if k in ('Wq', 'bq', 'Wk', 'bk', 'Wv', 'bv', 'Wo', 'bo')}
    del _L1_gnn_all
    return {'x': x, 'adj': adj, 'L0_gnn_Wq_w': _L0_gnn_in['Wq_w'], 'L0_gnn_Wq_b': _L0_gnn_in['Wq_b'], 'L0_gnn_Wk_w': _L0_gnn_in['Wk_w'], 'L0_gnn_Wk_b': _L0_gnn_in['Wk_b'], 'L0_gnn_Wv_w': _L0_gnn_in['Wv_w'], 'L0_gnn_Wv_b': _L0_gnn_in['Wv_b'], 'L1_gnn_Wq': _L1_gnn_in['Wq'], 'L1_gnn_bq': _L1_gnn_in['bq'], 'L1_gnn_Wk': _L1_gnn_in['Wk'], 'L1_gnn_bk': _L1_gnn_in['bk'], 'L1_gnn_Wv': _L1_gnn_in['Wv'], 'L1_gnn_bv': _L1_gnn_in['bv'], 'L1_gnn_Wo': _L1_gnn_in['Wo'], 'L1_gnn_bo': _L1_gnn_in['bo']}

def reference(x, adj, L0_gnn_Wq_w, L0_gnn_Wq_b, L0_gnn_Wk_w, L0_gnn_Wk_b, L0_gnn_Wv_w, L0_gnn_Wv_b, L1_gnn_Wq, L1_gnn_bq, L1_gnn_Wk, L1_gnn_bk, L1_gnn_Wv, L1_gnn_bv, L1_gnn_Wo, L1_gnn_bo):
    import jax
    import jax.numpy as jnp

    def _L0_gnn_ref(x, adj, Wq_w, Wq_b, Wk_w, Wk_b, Wv_w, Wv_b):
        import jax, jax.numpy as jnp
        import numpy as np
        B, N, D = (8, 1024, 256)
        query = jnp.einsum('bnd,od->bno', x, Wq_w) + Wq_b
        keyt = jnp.einsum('bnd,od->bno', x, Wk_w) + Wk_b
        value = jnp.einsum('bnd,od->bno', x, Wv_w) + Wv_b
        weight = jnp.einsum('bqd,bkd->bqk', query, keyt)
        weight = adj * jnp.exp(weight)
        weight = weight / jnp.sum(weight, axis=2, keepdims=True)
        return jnp.einsum('bqk,bkd->bqd', weight, value)

    def _L1_gnn_ref(x, adj_matrix, bond_matrix, Wq, bq, Wk, bk, Wv, bv, Wo, bo, seq_len):
        import jax, jax.numpy as jnp
        import numpy as np
        EMBED_DIM = 256
        NUM_HEADS = 8
        HEAD_DIM = EMBED_DIM // NUM_HEADS
        SCALE = HEAD_DIM ** (-0.5)
        B, S = (16, 512)
        b = x.shape[0]

        def proj(W, bias):
            y = jnp.einsum('bse,fe->bsf', x, W) + bias
            return y.reshape(b, seq_len, NUM_HEADS, HEAD_DIM).transpose(0, 2, 1, 3)
        q, k, v = (proj(Wq, bq), proj(Wk, bk), proj(Wv, bv))
        scores = jnp.einsum('bhqd,bhkd->bhqk', q, k) * SCALE
        mask = (adj_matrix + bond_matrix)[:, None, :, :]
        scores = scores * mask
        attn = jax.nn.softmax(scores, axis=-1)
        ctx = jnp.einsum('bhqk,bhkd->bhqd', attn, v)
        ctx = ctx.transpose(0, 2, 1, 3).reshape(b, seq_len, EMBED_DIM)
        return jnp.einsum('bse,fe->bsf', ctx, Wo) + bo
    x = _layernorm(x + _L0_gnn_ref(x, adj, L0_gnn_Wq_w, L0_gnn_Wq_b, L0_gnn_Wk_w, L0_gnn_Wk_b, L0_gnn_Wv_w, L0_gnn_Wv_b), axis=-1)
    x = _layernorm(x + _L1_gnn_ref(x, adj, adj, L1_gnn_Wq, L1_gnn_bq, L1_gnn_Wk, L1_gnn_bk, L1_gnn_Wv, L1_gnn_bv, L1_gnn_Wo, L1_gnn_bo, 256), axis=-1)
    return x

_drawn_inputs = setup_inputs


def setup_inputs(seed=0):
    import zlib

    import numpy as np

    out = dict(_drawn_inputs(seed))
    spreads = {'L0_gnn_Wq_b': (0.0, 0.1),
     'L0_gnn_Wk_b': (0.0, 0.8),
     'L0_gnn_Wv_b': (0.0, 0.1),
     'L1_gnn_bq': (0.0, 0.8),
     'L1_gnn_bk': (0.0, 0.8),
     'L1_gnn_bv': (0.0, 0.1),
     'L1_gnn_bo': (0.0, 0.1)}
    factors = {}
    for name, (base, spread) in spreads.items():
        noise = np.random.default_rng([zlib.crc32(name.encode()), seed]).standard_normal(out[name].shape)
        drawn = base * np.exp(spread * noise) if base else spread * noise
        out[name] = jnp.asarray(drawn.astype(out[name].dtype))
    for name, factor in factors.items():
        out[name] = (out[name] * factor).astype(out[name].dtype)
    return out
```

```python
from contextlib import ExitStack

import concourse.bass as bass
from concourse import mybir

F32 = mybir.dt.float32
F32R = mybir.dt.float32r
ALU = mybir.AluOpType
ACT = mybir.ActivationFunctionType

P = 128
B = 32
N = 256
D = 256
C = N // P
HEADS = 8
HD = D // HEADS
GROUPS = 2
PER_GROUP = HEADS // GROUPS
SCALE = 2.0 * float(HD) ** -0.5
EPS = 1e-5
LOWEST = -3.0e38
ACT_PT = (0, 1, 2, 4, 5, 6)


class Graph:

    def __init__(self, loop, offset):
        self.loop, self.offset = loop, offset
        self.parity = offset % 2
        self.peeled = isinstance(loop, int)

    def __add__(self, k):
        return Graph(self.loop, self.offset + k)

    @property
    def valid(self):
        return not self.peeled or 0 <= self.offset < B

    @property
    def index(self):
        return self.offset if self.peeled else self.loop * 2 + self.offset

    def count(self, n=1, k=None):
        k = n if k is None else k
        if self.peeled:
            return self.offset * n + k if self.offset < B else B * n
        return self.loop * (2 * n) + (self.offset * n + k)

    def count_of_parity(self, n=16):
        if self.peeled:
            return (self.offset // 2 + 1) * n
        return self.loop * n + (self.offset // 2 + 1) * n

    @property
    def started(self):
        return not self.peeled or self.offset >= 0


def build(nc, x, adj, wq0, bq0, wk0, bk0, wv0, bv0, wq1, bq1, wk1, bk1, wv1, bv1, wo1, bo1, out):
    ctx = ExitStack()
    with ctx:
        def sb(name, shape, dt=F32):
            return ctx.enter_context(nc.sbuf_tensor(name, [P, *shape], dt))

        def sem(name):
            return ctx.enter_context(nc.semaphore(name))

        weights = {"wq0": wq0, "wk0": wk0, "wv0": wv0, "wq1": wq1, "wk1": wk1, "wv1": wv1, "wo1": wo1}
        natural = {n: sb(n + "_sb", [C, D]) for n in weights}
        split_names = ("m0", "wv0", "wq1", "wk1", "wv1")
        w_hi = {n: sb(n + "_hi", [C, D], F32R) for n in split_names}
        w_lo = {n: sb(n + "_lo", [C, D], F32R) for n in split_names}
        woT = sb("woT", [C, D])
        ident = sb("ident", [P])
        bq0_col, bk0_col, bq1_col, bk1_col, bv1_col = (sb(n, [C]) for n in ("bq0_col", "bk0_col", "bq1_col", "bk1_col", "bv1_col"))
        bv0_row, bo1_row = sb("bv0_row", [D]), sb("bo1_row", [D])
        out_bias = sb("out_bias", [D])
        g_bias = sb("g_bias", [C])
        key_row = sb("key_row", [D])
        key_const = sb("key_const", [1])
        minus_half = sb("minus_half", [C])

        x_sb = [sb(f"x{i}", [C, D]) for i in range(2)]
        adj_front = [sb(f"adj_front{i}", [C, N]) for i in range(2)]
        x_plus = sb("x_plus", [C, D])
        xT_hi, xT_lo = sb("xT_hi", [C, N], F32R), sb("xT_lo", [C, N], F32R)
        g_hi, g_lo = sb("g_hi", [C, N], F32R), sb("g_lo", [C, N], F32R)
        v0_sb = sb("v0_sb", [C, D])
        row_dot = sb("row_dot", [C])
        row_bias = sb("row_bias", [C])
        scratch = sb("scratch", [C, D])
        p0 = sb("p0", [C, N])
        p0m = sb("p0m", [C, N])
        sum0, rsum0 = sb("sum0", [C]), sb("rsum0", [C])
        p0T_sb = sb("p0T_sb", [C, N])
        h0 = sb("h0", [C, D])
        x1 = [sb(f"x1_{i}", [C, D]) for i in range(2)]
        x1T_hi, x1T_lo = sb("x1T_hi", [C, N], F32R), sb("x1T_lo", [C, N], F32R)
        parts = sb("parts", [4, GROUPS, N], F32R)
        q_parts, k_parts = parts[:, 0:2], parts[:, 2:4]
        stacks = [sb(f"stacks{i}", [2, HEADS, N], F32R) for i in range(2)]
        v1_sb = [sb(f"v1_{i}", [C, D]) for i in range(2)]
        adj_heads = [sb(f"adj_heads{i}", [C, N]) for i in range(2)]
        masked = [sb(f"masked{i}", [C, N]) for i in range(2)]
        probs = [sb(f"probs{i}", [C, N]) for i in range(2)]
        pT_sb = [sb(f"pT{h}", [C, N]) for h in range(HEADS)]
        row_max = sb("row_max", [HEADS, C])
        neg_max = sb("neg_max", [HEADS, C])
        row_sum = [sb(f"row_sum{i}", [C, HEADS]) for i in range(2)]
        rsum = sb("rsum", [C, HEADS])
        rsum_wide = sb("rsum_wide", [C, D])
        r_sb = sb("r_sb", [GROUPS, N])
        oT_sb = sb("oT_sb", [GROUPS, N])
        x1_plus = [sb(f"x1_plus{i}", [C, D]) for i in range(2)]
        h1 = sb("h1", [C, D])
        out_sb = [sb(f"out{i}", [C, D]) for i in range(2)]
        stats = [sb(f"stats{i}", [C, 6]) for i in range(2)]
        mean_var = [sb(f"mean_var{i}", [C, 2]) for i in range(2)]
        var_eps, rstd, shift, neg_shift = ([sb(f"{n}{i}", [C]) for i in range(2)] for n in ("var_eps", "rstd", "shift", "neg_shift"))

        def bank(name):
            return ctx.enter_context(nc.psum_tensor(name, [P, 2, 256], F32))

        score_ps = [bank(f"score_ps{i}") for i in range(2)]
        pT_ps = [bank(f"pT_ps{i}") for i in range(2)]
        oT_ps = bank("oT_ps")
        work = [bank(f"work{i}") for i in range(3)]
        xT_ps, v0_ps, k_ps, p0T_ps = [work[0]] * 4
        g_ps, q_ps, r_ps, y_ps = [work[1]] * 4
        x1T_ps, s0_ps, v1_ps, a0_ps = [work[2]] * 4

        x_landed, adjf_landed, adjh_landed = ([sem(f"{n}{i}") for i in range(2)] for n in ("x_landed", "adjf_landed", "adjh_landed"))
        stacked = [[sem(f"stacked{i}_{r}") for r in range(PER_GROUP)] for i in range(2)]
        out_stored = [sem(f"out_stored{i}") for i in range(2)]
        weights_landed, ident_zero, consts_made = sem("weights_landed"), sem("ident_zero"), sem("consts_made")
        setup_ps_full, setup_hi, setup_copied = sem("setup_ps_full"), sem("setup_hi"), sem("setup_copied")
        xT_full, g_full, v0_full, s0_full, p0T_full, a0_full = (sem(n + "_full") for n in ("xT", "g", "v0", "s0", "p0T", "a0"))
        x1T_full, q_full, k_full, v1_full = (sem(n + "_full") for n in ("x1T", "q", "k", "v1"))
        score_full, pT_full, oT_full, r_full, y_full = (sem(n + "_full") for n in ("score", "pT", "oT", "r", "y"))
        xT_hi_done, xT_lo_done, g_hi_done, g_lo_done, v0_done = (sem(n + "_done") for n in ("xT_hi", "xT_lo", "g_hi", "g_lo", "v0"))
        row_dot_done, row_bias_done, p0_done, p0m_done, rsum0_done, p0T_done, h0_done = (
            sem(n + "_done") for n in ("row_dot", "row_bias", "p0", "p0m", "rsum0", "p0T", "h0"))
        x_plus_done, x1_done, x1_plus_done = sem("x_plus_done"), sem("x1_done"), sem("x1_plus_done")
        x1T_hi_done, x1T_lo_done, q_hi_done, q_lo_done, k_hi_done, k_lo_done, v1_done = (
            sem(n + "_done") for n in ("x1T_hi", "x1T_lo", "q_hi", "q_lo", "k_hi", "k_lo", "v1"))
        masked_done, neg_max_done, probs_done = sem("masked_done"), sem("neg_max_done"), sem("probs_done")
        pT_by_act, pT_by_dve = sem("pT_by_act"), sem("pT_by_dve")
        rsum_wide_done = sem("rsum_wide_done")
        rsum_done, r_done, oT_done, h1_done = sem("rsum_done"), sem("r_done"), sem("oT_done"), sem("h1_done")
        stats_done, mean_var_done, norm_chain = ([sem(f"{n}{i}") for i in range(2)] for n in ("stats_done", "mean_var_done", "norm_chain"))
        out_done = sem("out_done")

        f32 = lambda ap: ap.bitcast(F32)

        def by_parts(name, w):
            return w.rearrange("p (g r d) -> p r g d", g=GROUPS, d=HD) if name in ("wq1", "wk1") else w

        def by_heads(name, w):
            return w.rearrange("p (r g d) -> p r g d", g=GROUPS, d=HD) if name in ("wq1", "wk1") else w

        n_act = len(ACT_PT)
        n_dve = HEADS - n_act
        block = ctx.enter_context(nc.Block())

        SETUP = [*split_names, "wo1", "cols", "rows", "out_bias"]

        FIRST_LOOPED, PAIRS = 1, (B - 4) // 2

        def pipeline(eng, step):
            for t in range(-2, FIRST_LOOPED):
                step(Graph(0, t))
            with eng.Fori(0, PAIRS) as loop:
                for u in range(2):
                    step(Graph(loop, FIRST_LOOPED + u))
            for t in range(FIRST_LOOPED + 2 * PAIRS, B + 1):
                step(Graph(0, t))

        SETUP_LOADS = 7 + 3 + 2 * PER_GROUP + 2
        act_pt_before = [sum(1 for a in ACT_PT if a < h) for h in range(HEADS + 1)]

        @block.sync
        def _(sp):
            for n, w in weights.items():
                sp.dma_start(natural[n][:], w.rearrange("(c p) d -> p c d", p=P)).then_inc(weights_landed, 16)

            def load_x(g):
                sp.dma_start(x_sb[g.parity][:], x[g.index].rearrange("(c p) d -> p c d", p=P)).then_inc(x_landed[g.parity], 16)

            def load_adj(g, tiles, landed):
                sp.dma_start(tiles[g.parity][:], adj[g.index].rearrange("(c p) d -> p c d", p=P)).then_inc(landed[g.parity], 16)

            load_x(Graph(0, 0))
            load_adj(Graph(0, 0), adj_front, adjf_landed)
            with nc.allow_non_contiguous_dma(reason="a few hundred bias values, once"):
                for tile, b in ((bq0_col, bq0), (bk0_col, bk0), (bv1_col, bv1)):
                    sp.dma_start(tile[:], b.rearrange("(c p) -> p c", p=P)).then_inc(weights_landed, 16)
                for tile, b in ((bq1_col, bq1), (bk1_col, bk1)):
                    for r in range(PER_GROUP):
                        sp.dma_start(tile[HD * r:HD * r + HD, :], b.rearrange("(r g d) -> r d g", g=GROUPS, d=HD)[r]).then_inc(weights_landed, 16)
                for tile, b in ((bv0_row, bv0), (bo1_row, bo1)):
                    sp.dma_start(tile[:], b.rearrange("(a d) -> a d", a=1).to_broadcast([P, D])).then_inc(weights_landed, 16)

            def stack(g):
                for r in range(PER_GROUP):
                    for c, (q_part, k_part) in enumerate(((0, 2), (1, 3), (0, 3), (1, 2))):
                        sp.dma_start(f32(stacks[g.parity][HD * c:HD * c + HD, :, 2 * r:2 * r + 2, :]),
                                     f32(parts[HD * r:HD * r + HD, q_part:k_part + 1:k_part - q_part, :, :])).then_inc(stacked[g.parity][r], 16)

            def step(t):
                front, mid, tail = t + 2, t + 1, t + (-1)
                nxt = front + 1
                if nxt.valid:
                    if (nxt + (-2)).started:
                        sp.wait_ge(xT_full, (nxt + (-2)).count())
                        sp.nop(nofuse=True)
                        sp.wait_ge(row_dot_done, (nxt + (-2)).count(C))
                        sp.wait_ge(x_plus_done, (nxt + (-2)).count())
                    sp.nop(nofuse=True)
                    load_x(nxt)
                    if (nxt + (-2)).started:
                        sp.wait_ge(p0m_done, (nxt + (-2)).count(C))
                    sp.nop(nofuse=True)
                    load_adj(nxt, adj_front, adjf_landed)
                if mid.valid:
                    if (mid + (-2)).started:
                        sp.wait_ge(masked_done, (mid + (-2)).count(HEADS * C))
                    sp.nop(nofuse=True)
                    load_adj(mid, adj_heads, adjh_landed)
                    if (mid + (-2)).started:
                        sp.wait_ge(score_full, (mid + (-2)).count(HEADS))
                    sp.wait_ge(q_lo_done, mid.count(C))
                    sp.wait_ge(k_lo_done, mid.count(C))
                    sp.nop(nofuse=True)
                    stack(mid)
                if tail.valid:
                    sp.wait_ge(out_done, tail.count())
                    sp.nop(nofuse=True)
                    sp.dma_start(out[tail.index].rearrange("(c p) d -> p c d", p=P), out_sb[tail.parity][:]).then_inc(out_stored[tail.parity], 16)

            pipeline(sp, step)
            for i in range(2):
                sp.wait_ge(out_stored[i], 16 * (B // 2))

        @block.gpsimd
        def _(pool):
            nc.gpsimd.memset(ident[:], 0.0).then_inc(ident_zero, 1)
            nc.gpsimd.memset(minus_half[:], -0.5).then_inc(consts_made, 1)
            pool.wait_ge(ident_zero, 1)
            nc.gpsimd.affine_select(out=ident[:], in_=ident[:], compare_op=ALU.not_equal, fill=1.0, base=0,
                                    pattern=[[-1, P]], channel_multiplier=1).then_inc(consts_made, 1)
            pool.wait_ge(consts_made, 2)
            pool.wait_ge(weights_landed, 16 * SETUP_LOADS)

            def layer_norm(i, g, h, result, signal):
                pool.wait_ge(mean_var_done[i], g.count(C))
                pool.nop(nofuse=True)
                nc.gpsimd.tensor_scalar(var_eps[i][:], mean_var[i][:, :, 1], 1.0, EPS, ALU.mult, ALU.add).then_inc(norm_chain[i], 1)
                pool.wait_ge(norm_chain[i], g.count(4, 1))
                nc.gpsimd.tensor_tensor(rstd[i][:], var_eps[i][:], minus_half[:], ALU.pow).then_inc(norm_chain[i], 1)
                pool.wait_ge(norm_chain[i], g.count(4, 2))
                nc.gpsimd.tensor_tensor(shift[i][:], mean_var[i][:, :, 0], rstd[i][:], ALU.mult).then_inc(norm_chain[i], 1)
                pool.wait_ge(norm_chain[i], g.count(4, 3))
                pool.nop(nofuse=True)
                nc.gpsimd.tensor_scalar(neg_shift[i][:], shift[i][:], -1.0, 0.0, ALU.mult, ALU.add).then_inc(norm_chain[i], 1)
                pool.wait_ge(norm_chain[i], g.count(4, 4))
                pool.nop(nofuse=True)
                for c in range(C):
                    last = nc.gpsimd.tensor_scalar(result[:, c, :], h[:, c, :], rstd[i][:, c:c + 1], neg_shift[i][:, c:c + 1],
                                                   ALU.mult, ALU.add)
                last.then_inc(signal, 1)

            def step(t):
                front, mid, tail = t + 2, t + 1, t + (-1)
                if mid.valid:
                    if (mid + (-2)).started:
                        pool.wait_ge(x1_plus_done, (mid + (-2)).count())
                        pool.wait_ge(x1T_full, (mid + (-2)).count())
                    layer_norm(0, mid, h0, x1[mid.parity], x1_done)
                if front.valid:
                    pool.wait_ge(x_landed[front.parity], front.count_of_parity())
                    if (front + (-1)).started:
                        pool.wait_ge(h0_done, (front + (-1)).count(C))
                    for c in range(C):
                        last = nc.gpsimd.tensor_tensor(x_plus[:, c, :], x_sb[front.parity][:, c, :], bv0_row[:], ALU.add)
                    last.then_inc(x_plus_done, 1)
                if t.valid:
                    if t.peeled and t.offset == 0:
                        pool.wait_ge(setup_copied, len(SETUP))
                    pool.wait_ge(x1_done, t.count())
                    if (t + (-2)).started:
                        pool.wait_ge(h1_done, (t + (-2)).count(C))
                    for c in range(C):
                        last = nc.gpsimd.tensor_tensor(x1_plus[t.parity][:, c, :], x1[t.parity][:, c, :], out_bias[:], ALU.add)
                    last.then_inc(x1_plus_done, 1)
                if tail.valid:
                    pool.wait_ge(rsum_done, tail.count())
                    if (tail + (-1)).started:
                        pool.wait_ge(r_full, (tail + (-1)).count())
                    pool.nop(nofuse=True)
                    nc.gpsimd.tensor_scalar(rsum_wide[:].rearrange("p c (h d) -> p (c h) d", d=HD),
                                            rsum[:].rearrange("p c h -> p (c h)").unsqueeze(2).to_broadcast([P, C * HEADS, HD]),
                                            1.0, 0.0, ALU.mult, ALU.add).then_inc(rsum_wide_done, 1)
                    if (tail + (-2)).started:
                        pool.wait_ge(out_stored[tail.parity], (tail + (-2)).count_of_parity())
                    layer_norm(1, tail, h1, out_sb[tail.parity], out_done)

            pipeline(pool, step)

        @block.tensor
        def _(pe):
            def three_passes(dst, lhs, rhs, lhs_cols, rhs_cols=slice(0, D)):
                terms = [(lhs[a][:, k, lhs_cols], rhs[b][:, k, rhs_cols]) for k in range(C) for a, b in ((0, 0), (0, 1), (1, 0))]
                for n, (left, right) in enumerate(terms):
                    mm = nc.tensor.matmul(dst, left, right, start=(n == 0), stop=(n == len(terms) - 1))
                return mm

            def transposes(dst, src):
                for a in range(C):
                    for c in range(C):
                        mm = nc.tensor.transpose(dst[:, a, c * P:(c + 1) * P], src[:, c, a * P:(a + 1) * P], ident[:])
                return mm

            pe.wait_ge(consts_made, 2)
            pe.wait_ge(weights_landed, 16 * SETUP_LOADS)
            for i, name in enumerate(SETUP):
                ps = work[i % len(work)]
                if i >= 3:
                    pe.wait_ge(setup_copied, i - 2)
                if name == "m0":
                    for a in range(C):
                        for k in range(C):
                            mm = nc.tensor.matmul(ps[:, a, :], natural["wq0"][:, k, a * P:(a + 1) * P], natural["wk0"][:, k, :],
                                                  start=(k == 0), stop=(k == C - 1))
                elif name == "cols":
                    for a in range(C):
                        for k in range(C):
                            nc.tensor.matmul(ps[:, 0, a:a + 1], natural["wk0"][:, k, a * P:(a + 1) * P], bq0_col[:, k:k + 1],
                                             start=(k == 0), stop=(k == C - 1))
                    for k in range(C):
                        mm = nc.tensor.matmul(ps[:, 0, C:C + 1], bq0_col[:, k:k + 1].to_broadcast([P, P]), bk0_col[:, k:k + 1],
                                              start=(k == 0), stop=(k == C - 1))
                elif name == "rows":
                    for k in range(C):
                        mm = nc.tensor.matmul(ps[:, 0, :], bk0_col[:, k:k + 1].to_broadcast([P, P]), natural["wq0"][:, k, :],
                                              start=(k == 0), stop=(k == C - 1))
                elif name == "out_bias":
                    pe.wait_ge(setup_copied, SETUP.index("wo1") + 1)
                    for k in range(C):
                        mm = nc.tensor.matmul(ps[:, 0, :], bv1_col[:, k:k + 1].to_broadcast([P, P]), woT[:, k, :],
                                              start=(k == 0), stop=(k == C - 1))
                else:
                    mm = transposes(ps, natural[name])
                mm.then_inc(setup_ps_full, 1)
            pe.wait_ge(setup_copied, len(SETUP))

            def transpose_head(g, h):
                pe.wait_ge(probs_done, g.count(HEADS * C, (h + 1) * C))
                before, hb = (g, h - 2) if h >= 2 else (g + (-1), h + HEADS - 2)
                if before.started:
                    if hb in ACT_PT:
                        pe.wait_ge(pT_by_act, before.count(n_act, act_pt_before[hb + 1]))
                    else:
                        pe.wait_ge(pT_by_dve, before.count(n_dve, hb + 1 - act_pt_before[hb + 1]))
                transposes(pT_ps[h % 2], probs[h % 2]).then_inc(pT_full, 1)

            def attend(g, group):
                last = (group + 1) * PER_GROUP
                pe.wait_ge(pT_by_act, g.count(n_act, act_pt_before[last]))
                if last > act_pt_before[last]:
                    pe.wait_ge(pT_by_dve, g.count(n_dve, last - act_pt_before[last]))
                if group == 0:
                    pe.wait_ge(v1_done, g.count())
                    if (g + (-1)).started:
                        pe.wait_ge(oT_done, (g + (-1)).count())
                for k in range(C):
                    for r in range(PER_GROUP):
                        h = group * PER_GROUP + r
                        mm = nc.tensor.matmul(oT_ps[HD * r:HD * r + HD, group, :], v1_sb[g.parity][:, k, h * HD:(h + 1) * HD],
                                              pT_sb[h][:, k, :], start=(k == 0), stop=(k == C - 1), tile_position=(0, HD * r))
                mm.then_inc(oT_full, 1)

            def step(t):
                front, mid, tail = t + 2, t + 1, t + (-1)

                def scores(s):
                    if s % 2 == 0:
                        pe.wait_ge(stacked[t.parity][s // 2], t.count_of_parity(4 * 16))
                    before, hb = (t, s - 2) if s >= 2 else (t + (-1), s + HEADS - 2)
                    if before.started:
                        pe.wait_ge(masked_done, before.count(HEADS * C, (hb + 1) * C))
                    for c in range(C):
                        mm = nc.tensor.matmul(score_ps[s % 2][:, c, :], stacks[t.parity][:, 0, s, c * P:(c + 1) * P],
                                              stacks[t.parity][:, 1, s, :], start=True, stop=True)
                    mm.then_inc(score_full, 1)

                def front_xT():
                    pe.wait_ge(x_landed[front.parity], front.count_of_parity())
                    if (front + (-1)).started:
                        pe.wait_ge(p0T_done, (front + (-1)).count())
                    transposes(xT_ps, x_sb[front.parity]).then_inc(xT_full, 1)

                def front_g():
                    pe.wait_ge(xT_lo_done, front.count())
                    if (front + (-4)).started:
                        pe.wait_ge(h1_done, (front + (-4)).count(C))
                    for a in range(C):
                        mm = three_passes(g_ps[:, a, :], (w_hi["m0"], w_lo["m0"]), (xT_hi, xT_lo), slice(a * P, (a + 1) * P))
                    mm.then_inc(g_full, 1)

                def mid_x1T():
                    pe.wait_ge(x1_done, mid.count())
                    transposes(x1T_ps, x1[mid.parity]).then_inc(x1T_full, 1)

                def front_v0():
                    pe.wait_ge(xT_lo_done, front.count())
                    for a in range(C):
                        mm = three_passes(v0_ps[:, a, :], (xT_hi, xT_lo), (w_hi["wv0"], w_lo["wv0"]), slice(a * P, (a + 1) * P))
                    mm.then_inc(v0_full, 1)

                def mid_q():
                    pe.wait_ge(x1T_lo_done, mid.count())
                    pe.wait_ge(g_lo_done, front.count(C))
                    for a in range(C):
                        mm = three_passes(q_ps[:, a, :], (w_hi["wq1"], w_lo["wq1"]), (x1T_hi, x1T_lo), slice(a * P, (a + 1) * P))
                    mm.then_inc(q_full, 1)

                def front_s0():
                    pe.wait_ge(g_lo_done, front.count(C))
                    if (mid).started:
                        pe.wait_ge(x1T_lo_done, mid.count())
                    for c in range(C):
                        mm = three_passes(s0_ps[:, c, :], (g_hi, g_lo), (xT_hi, xT_lo), slice(c * P, (c + 1) * P))
                    mm.then_inc(s0_full, 1)

                def mid_k():
                    pe.wait_ge(v0_done, front.count())
                    for a in range(C):
                        mm = three_passes(k_ps[:, a, :], (w_hi["wk1"], w_lo["wk1"]), (x1T_hi, x1T_lo), slice(a * P, (a + 1) * P))
                    mm.then_inc(k_full, 1)

                def tail_r():
                    pe.wait_ge(rsum_wide_done, tail.count())
                    pe.wait_ge(q_lo_done, mid.count(C))
                    for gr in range(GROUPS):
                        for c in range(C):
                            mm = nc.tensor.transpose(
                                r_ps[:, gr, c * P:(c + 1) * P],
                                rsum_wide[:, c, gr * P:(gr + 1) * P], ident[:])
                    mm.then_inc(r_full, 1)

                def mid_v1():
                    if front.started:
                        pe.wait_ge(p0_done, front.count(C))
                    for a in range(C):
                        mm = three_passes(v1_ps[:, a, :], (x1T_hi, x1T_lo), (w_hi["wv1"], w_lo["wv1"]), slice(a * P, (a + 1) * P))
                    mm.then_inc(v1_full, 1)

                def front_p0T():
                    pe.wait_ge(p0m_done, front.count(C))
                    if mid.started:
                        pe.wait_ge(k_lo_done, mid.count(C))
                    transposes(p0T_ps, p0m).then_inc(p0T_full, 1)

                def tail_y():
                    pe.wait_ge(oT_done, tail.count())
                    for c in range(C):
                        for k in range(C):
                            mm = nc.tensor.matmul(y_ps[:, c, :], oT_sb[:, k, c * P:(c + 1) * P], woT[:, k, :],
                                                  start=(k == 0), stop=(k == C - 1))
                    mm.then_inc(y_full, 1)

                def front_a0():
                    pe.wait_ge(p0T_done, front.count())
                    if mid.started:
                        pe.wait_ge(v1_done, mid.count())
                    for c in range(C):
                        for k in range(C):
                            mm = nc.tensor.matmul(a0_ps[:, c, :], p0T_sb[:, k, c * P:(c + 1) * P], v0_sb[:, k, :],
                                                  start=(k == 0), stop=(k == C - 1))
                    mm.then_inc(a0_full, 1)

                for s in range(HEADS):
                    if t.valid:
                        scores(s)
                    if s == 0 and front.valid:
                        front_xT()
                    if s == 1 and front.valid:
                        front_g()
                    if s == 2 and mid.valid:
                        mid_x1T()
                    if s == 3 and mid.valid:
                        mid_q()
                    if s == 4 and mid.valid:
                        mid_k()
                    if s == 5 and mid.valid:
                        mid_v1()
                    if s == 6 and tail.valid:
                        tail_y()
                    if s == 7 and front.valid:
                        front_a0()
                    if s >= 1 and t.valid:
                        transpose_head(t, s - 1)
                    if s == 0 and tail.valid:
                        transpose_head(tail, HEADS - 1)
                    if s == 1 and tail.valid:
                        attend(tail, 1)
                    if s == 2 and front.valid:
                        front_v0()
                    if s == 3 and front.valid:
                        front_s0()
                    if s == 4 and tail.valid:
                        tail_r()
                    if s == 5 and front.valid:
                        front_p0T()
                    if s == 6 and t.valid:
                        attend(t, 0)

            pipeline(pe, step)

        @block.scalar
        def _(act):
            for i, name in enumerate(split_names):
                act.wait_ge(setup_ps_full, i + 1)
                for a in range(C):
                    last = nc.scalar.copy(by_parts(name, w_hi[name][:, a, :]), by_heads(name, work[i % len(work)][:, a, :]))
                last.then_inc(setup_hi, 1)
            act.wait_ge(setup_copied, len(SETUP))

            def head_exp(g, h):
                for c in range(C):
                    act.wait_ge(neg_max_done, g.count(HEADS, h + 1))
                    if c == 0:
                        before, hb = (g, h - 2) if h >= 2 else (g + (-1), h + HEADS - 2)
                        if before.started:
                            act.wait_ge(pT_full, before.count(HEADS, hb + 1))
                        if h == 0 and (g + (-2)).started:
                            act.wait_ge(rsum_done, (g + (-2)).count())
                    nc.scalar.activation(probs[h % 2][:, c, :], masked[h % 2][:, c, :], ACT.Exp, bias=neg_max[:, h, c:c + 1],
                                         scale=SCALE, accum_out=row_sum[g.parity][:, c, h:h + 1]).then_inc(probs_done, 1)

            def copy_pT(g, h):
                if h not in ACT_PT:
                    return
                act.wait_ge(pT_full, g.count(HEADS, h + 1))
                nc.scalar.copy(pT_sb[h][:], pT_ps[h % 2][:]).then_inc(pT_by_act, 1)

            def step(t):
                front, mid, tail = t + 2, t + 1, t + (-1)
                for s in range(HEADS):
                    if t.valid:
                        head_exp(t, s)
                    if s == 0 and front.valid:
                        act.wait_ge(xT_full, front.count())
                        nc.scalar.copy(xT_hi[:], xT_ps[:]).then_inc(xT_hi_done, 1)
                    if s == 1 and front.valid:
                        act.wait_ge(g_full, front.count())
                        for a in range(C):
                            nc.scalar.activation(g_hi[:, a, :], g_ps[:, a, :], ACT.Identity, bias=g_bias[:, a:a + 1]).then_inc(g_hi_done, 1)
                    if s == 2 and mid.valid:
                        act.wait_ge(x1T_full, mid.count())
                        nc.scalar.copy(x1T_hi[:], x1T_ps[:]).then_inc(x1T_hi_done, 1)
                    if s == 3 and mid.valid:
                        act.wait_ge(q_full, mid.count())
                        if (mid + (-1)).started:
                            pm = mid + (-1)
                            for r in range(PER_GROUP):
                                act.wait_ge(stacked[pm.parity][r], pm.count_of_parity(4 * 16))
                        for a in range(C):
                            nc.scalar.activation(q_parts[:, 0, a, :], q_ps[:, a, :], ACT.Identity, bias=bq1_col[:, a:a + 1]).then_inc(q_hi_done, 1)
                    if s == 4 and mid.valid:
                        act.wait_ge(k_full, mid.count())
                        for a in range(C):
                            nc.scalar.activation(k_parts[:, 0, a, :], k_ps[:, a, :], ACT.Identity, bias=bk1_col[:, a:a + 1]).then_inc(k_hi_done, 1)
                    if s == 5 and mid.valid:
                        act.wait_ge(v1_full, mid.count())
                        nc.scalar.copy(v1_sb[mid.parity][:], v1_ps[:]).then_inc(v1_done, 1)
                    if s >= 1 and t.valid:
                        copy_pT(t, s - 1)
                    if s == 0 and tail.valid:
                        copy_pT(tail, HEADS - 1)
                    if s == 2 and front.valid:
                        act.wait_ge(v0_full, front.count())
                        nc.scalar.copy(v0_sb[:], v0_ps[:]).then_inc(v0_done, 1)
                    if s == 3 and front.valid:
                        act.wait_ge(s0_full, front.count())
                        act.wait_ge(row_bias_done, front.count())
                        for c in range(C):
                            nc.scalar.activation(p0[:, c, :], s0_ps[:, c, :], ACT.Exp, bias=row_bias[:, c:c + 1]).then_inc(p0_done, 1)
                    if s == 4 and tail.valid:
                        act.wait_ge(r_full, tail.count())
                        nc.scalar.copy(r_sb[:], r_ps[:]).then_inc(r_done, 1)
                    if s == 5 and front.valid:
                        act.wait_ge(p0T_full, front.count())
                        nc.scalar.copy(p0T_sb[:], p0T_ps[:]).then_inc(p0T_done, 1)

            pipeline(act, step)

        @block.vector
        def _(dve):
            dve.wait_ge(weights_landed, 16 * SETUP_LOADS)
            for i, name in enumerate(SETUP):
                ps = work[i % len(work)]
                dve.wait_ge(setup_ps_full, i + 1)
                if name in split_names:
                    dve.wait_ge(setup_hi, i + 1)
                    for a in range(C):
                        last = nc.vector.tensor_tensor(by_parts(name, w_lo[name][:, a, :]), by_heads(name, ps[:, a, :]),
                                                       by_parts(name, f32(w_hi[name][:, a, :])), ALU.subtract)
                elif name == "wo1":
                    last = nc.vector.tensor_copy(woT[:], ps[:])
                elif name == "cols":
                    nc.vector.tensor_copy(g_bias[:], ps[:, 0, 0:C])
                    last = nc.vector.tensor_copy(key_const[:], ps[:, 0, C:C + 1])
                elif name == "rows":
                    last = nc.vector.tensor_copy(key_row[:], ps[:, 0, :])
                else:
                    last = nc.vector.tensor_tensor(out_bias[:], ps[:, 0, :], bo1_row[:], ALU.add)
                last.then_inc(setup_copied, 1)
            dve.wait_ge(setup_copied, len(SETUP))

            def lo_part(lo, ps, hi, bias=None):
                if bias is None:
                    return [nc.vector.tensor_tensor(lo, ps, f32(hi), ALU.subtract)]
                return [nc.vector.scalar_tensor_tensor(out=lo[:, a, :], in0=ps[:, a, :], scalar=bias[:, a:a + 1], in1=f32(hi[:, a, :]),
                                                       op0=ALU.add, op1=ALU.subtract) for a in range(C)]

            def head_mask(g, h):
                dve.wait_ge(score_full, g.count(HEADS, h + 1))
                if h == 0:
                    dve.wait_ge(adjh_landed[g.parity], g.count_of_parity())
                before, hb = (g, h - 2) if h >= 2 else (g + (-1), h + HEADS - 2)
                if before.started:
                    dve.wait_ge(probs_done, before.count(HEADS * C, (hb + 1) * C))
                dve.nop(nofuse=True)
                for c in range(C):
                    nc.vector.tensor_tensor_reduce(masked[h % 2][:, c, :], score_ps[h % 2][:, c, :], adj_heads[g.parity][:, c, :],
                                                   1.0, LOWEST, ALU.mult, ALU.max, row_max[:, h, c:c + 1]).then_inc(masked_done, 1)
                dve.wait_ge(masked_done, g.count(HEADS * C, (h + 1) * C))
                nc.vector.tensor_scalar(neg_max[:, h, :], row_max[:, h, :], -SCALE, None, ALU.mult).then_inc(neg_max_done, 1)

            def copy_pT(g, h):
                if h in ACT_PT:
                    return
                dve.wait_ge(pT_full, g.count(HEADS, h + 1))
                nc.vector.tensor_copy(pT_sb[h][:], pT_ps[h % 2][:]).then_inc(pT_by_dve, 1)

            def residual_stats(i, g, h, ps, scale, plus, signal, norm_done):
                if (g + (-1)).started:
                    dve.wait_ge(norm_done, (g + (-1)).count())
                for c in range(C):
                    if scale is None:
                        nc.vector.tensor_tensor(h[:, c, :], ps[:, c, :], plus[:, c, :], ALU.add).then_inc(signal, 1)
                    else:
                        nc.vector.scalar_tensor_tensor(out=h[:, c, :], in0=ps[:, c, :], scalar=scale[:, c:c + 1], in1=plus[:, c, :],
                                                       op0=ALU.mult, op1=ALU.add).then_inc(signal, 1)
                for c in range(C):
                    dve.wait_ge(signal, g.count(C, c + 1))
                    nc.vector.bn_stats(stats[i][:, c, :], h[:, c, :]).then_inc(stats_done[i], 1)
                for c in range(C):
                    dve.wait_ge(stats_done[i], g.count(C, c + 1))
                    dve.nop(nofuse=True)
                    nc.vector.bn_aggr(mean_var[i][:, c, :], stats[i][:, c, :]).then_inc(mean_var_done[i], 1)

            def step(t):
                front, mid, tail = t + 2, t + 1, t + (-1)
                for s in range(HEADS):
                    if t.valid:
                        head_mask(t, s)
                    if s == 0 and mid.valid:
                        dve.wait_ge(a0_full, mid.count())
                        dve.wait_ge(x_plus_done, mid.count())
                        dve.wait_ge(rsum0_done, mid.count())
                        residual_stats(0, mid, h0, a0_ps, rsum0, x_plus, h0_done, x1_done)
                    if s == 0 and front.valid:
                        dve.wait_ge(xT_full, front.count())
                        dve.wait_ge(xT_hi_done, front.count())
                        lo_part(xT_lo[:], xT_ps[:], xT_hi[:])[-1].then_inc(xT_lo_done, 1)
                    if s == 1 and front.valid:
                        dve.wait_ge(g_hi_done, front.count(C))
                        for op in lo_part(g_lo, g_ps, g_hi, g_bias):
                            op.then_inc(g_lo_done, 1)
                        dve.wait_ge(x_landed[front.parity], front.count_of_parity())
                        if (front + (-1)).started:
                            dve.wait_ge(row_bias_done, (front + (-1)).count())
                        for c in range(C):
                            nc.vector.tensor_tensor_reduce(scratch[:, c, :], x_sb[front.parity][:, c, :], key_row[:], 1.0, 0.0,
                                                           ALU.mult, ALU.add, row_dot[:, c:c + 1]).then_inc(row_dot_done, 1)
                        dve.wait_ge(row_dot_done, front.count(C))
                        if (front + (-1)).started:
                            dve.wait_ge(p0_done, (front + (-1)).count(C))
                        nc.vector.tensor_scalar(row_bias[:], row_dot[:], key_const[:, 0:1], None, ALU.add).then_inc(row_bias_done, 1)
                    if s == 2 and mid.valid:
                        dve.wait_ge(x1T_hi_done, mid.count())
                        lo_part(x1T_lo[:], x1T_ps[:], x1T_hi[:])[-1].then_inc(x1T_lo_done, 1)
                    if s == 3 and mid.valid:
                        dve.wait_ge(q_hi_done, mid.count(C))
                        for op in lo_part(q_parts[:, 1], q_ps, q_parts[:, 0], bq1_col):
                            op.then_inc(q_lo_done, 1)
                    if s == 3 and tail.valid:
                        dve.wait_ge(probs_done, tail.count(HEADS * C))
                        nc.vector.reciprocal(rsum[:], row_sum[tail.parity][:]).then_inc(rsum_done, 1)
                    if s == 4 and front.valid:
                        dve.wait_ge(adjf_landed[front.parity], front.count_of_parity())
                        for c in range(C):
                            dve.wait_ge(p0_done, front.count(C, c + 1))
                            nc.vector.tensor_tensor_reduce(p0m[:, c, :], p0[:, c, :], adj_front[front.parity][:, c, :], 1.0, 0.0,
                                                           ALU.mult, ALU.add, sum0[:, c:c + 1]).then_inc(p0m_done, 1)
                        dve.wait_ge(p0m_done, front.count(C))
                        nc.vector.reciprocal(rsum0[:], sum0[:]).then_inc(rsum0_done, 1)
                    if s == 4 and mid.valid:
                        dve.wait_ge(k_hi_done, mid.count(C))
                        for op in lo_part(k_parts[:, 1], k_ps, k_parts[:, 0], bk1_col):
                            op.then_inc(k_lo_done, 1)
                    if s == 5 and tail.valid:
                        dve.wait_ge(r_done, tail.count())
                        dve.wait_ge(oT_full, tail.count(GROUPS))
                        nc.vector.tensor_tensor(oT_sb[:], oT_ps[:], r_sb[:], ALU.mult).then_inc(oT_done, 1)
                    if s >= 1 and t.valid:
                        copy_pT(t, s - 1)
                    if s == 0 and tail.valid:
                        copy_pT(tail, HEADS - 1)
                    if s == 7 and tail.valid:
                        dve.wait_ge(y_full, tail.count())
                        dve.wait_ge(x1_plus_done, tail.count())
                        residual_stats(1, tail, h1, y_ps, None, x1_plus[tail.parity], h1_done, out_done)

            pipeline(dve, step)


INPUTS = ["x", "adj", "L0_gnn_Wq_w", "L0_gnn_Wq_b", "L0_gnn_Wk_w", "L0_gnn_Wk_b", "L0_gnn_Wv_w", "L0_gnn_Wv_b",
          "L1_gnn_Wq", "L1_gnn_bq", "L1_gnn_Wk", "L1_gnn_bk", "L1_gnn_Wv", "L1_gnn_bv", "L1_gnn_Wo", "L1_gnn_bo"]


def kernel(**inputs):
    import numpy as np
    import concourse.bacc as bacc
    from concourse.bass_utils import run_bass_kernel_spmd

    nc = bacc.Bacc("TRN2", target_bir_lowering=False, num_devices=1)
    arrays, args = {}, []
    for name in INPUTS:
        a = np.ascontiguousarray(inputs[name])
        arrays[f"in_{name}"] = a
        args.append(nc.dram_tensor(f"in_{name}", a.shape, mybir.dt.from_np(a.dtype), kind="ExternalInput").ap())
    out = nc.dram_tensor("out_x", (B, N, D), F32, kind="ExternalOutput").ap()
    build(nc, *args, out)
    r = run_bass_kernel_spmd(nc, [arrays], core_ids=[0])
    return r.results[0]["out_x"]
```

```python
from contextlib import ExitStack

import concourse.bass as bass
from concourse import mybir

F32 = mybir.dt.float32
F32R = mybir.dt.float32r
ALU = mybir.AluOpType
ACT = mybir.ActivationFunctionType

P = 128
B = 32
N = 256
D = 256
C = N // P
HEADS = 8
HD = D // HEADS
GROUPS = 2
PER_GROUP = HEADS // GROUPS
SCALE = 2.0 * float(HD) ** -0.5
EPS = 1e-5
LOWEST = -3.0e38
LAG = 2
RING = 4
ACT_PT = (0, 1, 2, 4, 6, 7)

TENSOR_ORDER = """
scores:0 v1 transpose:0
scores:1 g transpose:1
scores:2 x1T attend_last transpose:2 r
scores:3 q transpose:3 s0
scores:4 k transpose:4 v0
scores:5 y transpose:5
scores:6 p0T transpose:6 attend_first
scores:7 xT transpose:7 a0
"""
SCALAR_ORDER = """
v1 exp:0 copy:0
g copy:1 exp:1
x1T exp:2 copy:2 r
exp:3 q copy:3
p0 exp:4 k copy:4
v0 exp:5 copy:5
p0T exp:6 copy:6
xT exp:7 copy:7
"""
VECTOR_ORDER = """
mask:0 stats0 copy:0
mask:1 rsum norm0 g copy:1
mask:2 x1T rows copy:2
mask:3 q oT copy:3
mask:4 p0m k copy:4
mask:5 copy:5
mask:6 h1 stats1 copy:6
mask:7 xT copy:7 h0
"""
GPSIMD_ORDER = "rstd0 x_plus rsum_wide x1_plus rstd1 norm1"


class Graph:

    def __init__(self, loop, offset):
        self.loop, self.offset = loop, offset
        self.parity = offset % 2
        self.peeled = isinstance(loop, int)

    def __add__(self, k):
        return Graph(self.loop, self.offset + k)

    @property
    def valid(self):
        return not self.peeled or 0 <= self.offset < B

    @property
    def index(self):
        return self.offset if self.peeled else self.loop * 2 + self.offset

    def count(self, n=1, k=None):
        k = n if k is None else k
        if self.peeled:
            return self.offset * n + k if self.offset < B else B * n
        return self.loop * (2 * n) + (self.offset * n + k)

    def count_of_parity(self, n=16):
        if self.peeled:
            return (self.offset // 2 + 1) * n
        return self.loop * n + (self.offset // 2 + 1) * n

    @property
    def started(self):
        return not self.peeled or self.offset >= 0


def build(nc, x, adj, wq0, bq0, wk0, bk0, wv0, bv0, wq1, bq1, wk1, bk1, wv1, bv1, wo1, bo1, out):
    ctx = ExitStack()
    with ctx:
        def sb(name, shape, dt=F32):
            return ctx.enter_context(nc.sbuf_tensor(name, [P, *shape], dt))

        def sem(name):
            return ctx.enter_context(nc.semaphore(name))

        weights = {"wq0": wq0, "wk0": wk0, "wv0": wv0, "wq1": wq1, "wk1": wk1, "wv1": wv1, "wo1": wo1}
        natural = {n: sb(n + "_sb", [C, D]) for n in weights}
        split_names = ("m0", "wv0", "wq1", "wk1", "wv1")
        w_hi = {n: sb(n + "_hi", [C, D], F32R) for n in split_names}
        w_lo = {n: sb(n + "_lo", [C, D], F32R) for n in split_names}
        woT = sb("woT", [C, D])
        ident = sb("ident", [P])
        bq0_col, bk0_col, bq1_col, bk1_col, bv1_col = (sb(n, [C]) for n in ("bq0_col", "bk0_col", "bq1_col", "bk1_col", "bv1_col"))
        bv0_row, bo1_row = sb("bv0_row", [D]), sb("bo1_row", [D])
        out_bias = sb("out_bias", [D])
        g_bias = sb("g_bias", [C])
        key_row = sb("key_row", [D])
        key_const = sb("key_const", [1])
        minus_half = sb("minus_half", [C])

        x_sb = [sb(f"x{i}", [C, D]) for i in range(2)]
        adj_front = [sb(f"adj_front{i}", [C, N]) for i in range(2)]
        x_plus = sb("x_plus", [C, D])
        xT_hi, xT_lo = sb("xT_hi", [C, N], F32R), sb("xT_lo", [C, N], F32R)
        g_hi, g_lo = sb("g_hi", [C, N], F32R), sb("g_lo", [C, N], F32R)
        v0_sb = sb("v0_sb", [C, D])
        row_dot = sb("row_dot", [C])
        row_bias = sb("row_bias", [C])
        scratch = sb("scratch", [C, D])
        p0 = sb("p0", [C, N])
        p0m = sb("p0m", [C, N])
        sum0, rsum0 = sb("sum0", [C]), sb("rsum0", [C])
        p0T_sb = sb("p0T_sb", [C, N])
        h0 = sb("h0", [C, D])
        x1 = [sb(f"x1_{i}", [C, D]) for i in range(2)]
        x1T_hi, x1T_lo = sb("x1T_hi", [C, N], F32R), sb("x1T_lo", [C, N], F32R)
        parts = sb("parts", [4, GROUPS, N], F32R)
        q_parts, k_parts = parts[:, 0:2], parts[:, 2:4]
        stacks = [sb(f"stacks{i}", [2, HEADS, N], F32R) for i in range(2)]
        v1_sb = [sb(f"v1_{i}", [C, D]) for i in range(2)]
        adj_heads = [sb(f"adj_heads{i}", [C, N]) for i in range(2)]
        masked = [sb(f"masked{i}", [C, N]) for i in range(RING)]
        probs = [sb(f"probs{i}", [C, N]) for i in range(RING)]
        pT_sb = [sb(f"pT{h}", [C, N]) for h in range(HEADS)]
        row_max = sb("row_max", [HEADS, C])
        neg_max = sb("neg_max", [HEADS, C])
        row_sum = [sb(f"row_sum{i}", [C, HEADS]) for i in range(2)]
        rsum = sb("rsum", [C, HEADS])
        rsum_wide = sb("rsum_wide", [C, D])
        r_sb = sb("r_sb", [GROUPS, N])
        oT_sb = sb("oT_sb", [GROUPS, N])
        x1_plus = [sb(f"x1_plus{i}", [C, D]) for i in range(2)]
        h1 = sb("h1", [C, D])
        out_sb = [sb(f"out{i}", [C, D]) for i in range(2)]
        stats = [sb(f"stats{i}", [C, 6]) for i in range(2)]
        mean_var = [sb(f"mean_var{i}", [C, 2]) for i in range(2)]
        var_eps, rstd = ([sb(f"{n}{i}", [C]) for i in range(2)] for n in ("var_eps", "rstd"))
        shift, neg_shift = sb("shift", [C]), sb("neg_shift", [C])

        def bank(name):
            return ctx.enter_context(nc.psum_tensor(name, [P, 2, 256], F32))

        score_ps = [bank(f"score_ps{i}") for i in range(2)]
        pT_ps = [bank(f"pT_ps{i}") for i in range(2)]
        oT_ps = bank("oT_ps")
        work = [bank(f"work{i}") for i in range(3)]
        v1_ps, r_ps, k_ps, p0T_ps = [work[0]] * 4
        g_ps, q_ps, v0_ps, xT_ps = [work[1]] * 4
        x1T_ps, s0_ps, y_ps, a0_ps = [work[2]] * 4

        x_landed, adjf_landed, adjh_landed = ([sem(f"{n}{i}") for i in range(2)] for n in ("x_landed", "adjf_landed", "adjh_landed"))
        stacked = [[sem(f"stacked{i}_{r}") for r in range(PER_GROUP)] for i in range(2)]
        out_stored = [sem(f"out_stored{i}") for i in range(2)]
        weights_landed, ident_zero, consts_made = sem("weights_landed"), sem("ident_zero"), sem("consts_made")
        setup_ps_full, setup_hi, setup_copied = sem("setup_ps_full"), sem("setup_hi"), sem("setup_copied")
        xT_full, g_full, v0_full, s0_full, p0T_full, a0_full = (sem(n + "_full") for n in ("xT", "g", "v0", "s0", "p0T", "a0"))
        x1T_full, q_full, k_full, v1_full = (sem(n + "_full") for n in ("x1T", "q", "k", "v1"))
        score_full, pT_full, oT_full, r_full, y_full = (sem(n + "_full") for n in ("score", "pT", "oT", "r", "y"))
        xT_hi_done, xT_lo_done, g_hi_done, g_lo_done, v0_done = (sem(n + "_done") for n in ("xT_hi", "xT_lo", "g_hi", "g_lo", "v0"))
        row_dot_done, row_bias_done, p0_done, p0m_done, rsum0_done, p0T_done, h0_done = (
            sem(n + "_done") for n in ("row_dot", "row_bias", "p0", "p0m", "rsum0", "p0T", "h0"))
        x_plus_done, x1_done, x1_plus_done = sem("x_plus_done"), sem("x1_done"), sem("x1_plus_done")
        x1T_hi_done, x1T_lo_done, q_hi_done, q_lo_done, k_hi_done, k_lo_done, v1_done = (
            sem(n + "_done") for n in ("x1T_hi", "x1T_lo", "q_hi", "q_lo", "k_hi", "k_lo", "v1"))
        masked_done, neg_max_done, probs_done = sem("masked_done"), sem("neg_max_done"), sem("probs_done")
        pT_by_act, pT_by_dve = sem("pT_by_act"), sem("pT_by_dve")
        rsum_wide_done = sem("rsum_wide_done")
        rsum_done, r_done, oT_done, h1_done = sem("rsum_done"), sem("r_done"), sem("oT_done"), sem("h1_done")
        stats_done, mean_var_done, var_eps_done, rstd_done = (
            [sem(f"{n}{i}") for i in range(2)] for n in ("stats_done", "mean_var_done", "var_eps_done", "rstd_done"))
        shift_done, neg_shift_done = sem("shift_done"), sem("neg_shift_done")
        out_done = sem("out_done")

        f32 = lambda ap: ap.bitcast(F32)

        def by_parts(name, w):
            return w.rearrange("p (g r d) -> p r g d", g=GROUPS, d=HD) if name in ("wq1", "wk1") else w

        def by_heads(name, w):
            return w.rearrange("p (r g d) -> p r g d", g=GROUPS, d=HD) if name in ("wq1", "wk1") else w

        n_act = len(ACT_PT)
        n_dve = HEADS - n_act
        block = ctx.enter_context(nc.Block())

        SETUP = [*split_names, "wo1", "cols", "rows", "out_bias"]

        FIRST_LOOPED, PAIRS = 1, (B - 4) // 2

        def pipeline(eng, step):
            for t in range(-3, FIRST_LOOPED):
                step(Graph(0, t))
            with eng.Fori(0, PAIRS) as loop:
                for u in range(2):
                    step(Graph(loop, FIRST_LOOPED + u))
            for t in range(FIRST_LOOPED + 2 * PAIRS, B + 1):
                step(Graph(0, t))

        def lagging(t, n):
            return (t, n - LAG) if n >= LAG else (t + (-1), n + HEADS - LAG)

        SETUP_LOADS = 7 + 3 + 2 * PER_GROUP + 2
        act_pt_before = [sum(1 for a in ACT_PT if a < h) for h in range(HEADS + 1)]

        @block.sync
        def _(sp):
            for n, w in weights.items():
                sp.dma_start(natural[n][:], w.rearrange("(c p) d -> p c d", p=P)).then_inc(weights_landed, 16)

            def load_x(g):
                sp.dma_start(x_sb[g.parity][:], x[g.index].rearrange("(c p) d -> p c d", p=P)).then_inc(x_landed[g.parity], 16)

            def load_adj(g, tiles, landed):
                sp.dma_start(tiles[g.parity][:], adj[g.index].rearrange("(c p) d -> p c d", p=P)).then_inc(landed[g.parity], 16)

            with nc.allow_non_contiguous_dma(reason="a few hundred bias values, once"):
                for tile, b in ((bq0_col, bq0), (bk0_col, bk0), (bv1_col, bv1)):
                    sp.dma_start(tile[:], b.rearrange("(c p) -> p c", p=P)).then_inc(weights_landed, 16)
                for tile, b in ((bq1_col, bq1), (bk1_col, bk1)):
                    for r in range(PER_GROUP):
                        sp.dma_start(tile[HD * r:HD * r + HD, :], b.rearrange("(r g d) -> r d g", g=GROUPS, d=HD)[r]).then_inc(weights_landed, 16)
                for tile, b in ((bv0_row, bv0), (bo1_row, bo1)):
                    sp.dma_start(tile[:], b.rearrange("(a d) -> a d", a=1).to_broadcast([P, D])).then_inc(weights_landed, 16)

            def stack(g):
                for r in range(PER_GROUP):
                    for c, (q_part, k_part) in enumerate(((0, 2), (1, 3), (0, 3), (1, 2))):
                        sp.dma_start(f32(stacks[g.parity][HD * c:HD * c + HD, :, 2 * r:2 * r + 2, :]),
                                     f32(parts[HD * r:HD * r + HD, q_part:k_part + 1:k_part - q_part, :, :])).then_inc(stacked[g.parity][r], 16)

            def step(t):
                front, mid, tail = t + 2, t + 1, t + (-1)
                nxt = front + 1
                if nxt.valid:
                    if (nxt + (-2)).started:
                        sp.wait_ge(xT_full, (nxt + (-2)).count())
                        sp.nop(nofuse=True)
                        sp.wait_ge(row_dot_done, (nxt + (-2)).count(C))
                        sp.wait_ge(x_plus_done, (nxt + (-2)).count())
                    sp.nop(nofuse=True)
                    load_x(nxt)
                    if (nxt + (-2)).started:
                        sp.wait_ge(p0m_done, (nxt + (-2)).count(C))
                    sp.nop(nofuse=True)
                    load_adj(nxt, adj_front, adjf_landed)
                if mid.valid:
                    if (mid + (-2)).started:
                        sp.wait_ge(masked_done, (mid + (-2)).count(HEADS * C))
                    sp.nop(nofuse=True)
                    load_adj(mid, adj_heads, adjh_landed)
                    if (mid + (-2)).started:
                        sp.wait_ge(score_full, (mid + (-2)).count(HEADS))
                    sp.wait_ge(q_lo_done, mid.count(C))
                    sp.wait_ge(k_lo_done, mid.count(C))
                    sp.nop(nofuse=True)
                    stack(mid)
                if tail.valid:
                    sp.wait_ge(out_done, tail.count())
                    sp.nop(nofuse=True)
                    sp.dma_start(out[tail.index].rearrange("(c p) d -> p c d", p=P), out_sb[tail.parity][:]).then_inc(out_stored[tail.parity], 16)

            pipeline(sp, step)
            for i in range(2):
                sp.wait_ge(out_stored[i], 16 * (B // 2))

        @block.gpsimd
        def _(pool):
            nc.gpsimd.memset(ident[:], 0.0).then_inc(ident_zero, 1)
            nc.gpsimd.memset(minus_half[:], -0.5).then_inc(consts_made, 1)
            pool.wait_ge(ident_zero, 1)
            nc.gpsimd.affine_select(out=ident[:], in_=ident[:], compare_op=ALU.not_equal, fill=1.0, base=0,
                                    pattern=[[-1, P]], channel_multiplier=1).then_inc(consts_made, 1)
            pool.wait_ge(consts_made, 2)
            pool.wait_ge(weights_landed, 16 * SETUP_LOADS)

            def inverse_deviation(i, g):
                pool.wait_ge(mean_var_done[i], g.count(C))
                pool.nop(nofuse=True)
                nc.gpsimd.tensor_scalar(var_eps[i][:], mean_var[i][:, :, 1], 1.0, EPS, ALU.mult, ALU.add).then_inc(var_eps_done[i], 1)
                pool.wait_ge(var_eps_done[i], g.count())
                nc.gpsimd.tensor_tensor(rstd[i][:], var_eps[i][:], minus_half[:], ALU.pow).then_inc(rstd_done[i], 1)

            def normalise(i, g, h, result, signal):
                pool.wait_ge(rstd_done[i], g.count())
                nc.gpsimd.tensor_tensor(shift[:], mean_var[i][:, :, 0], rstd[i][:], ALU.mult).then_inc(shift_done, 1)
                pool.wait_ge(shift_done, g.count())
                pool.nop(nofuse=True)
                nc.gpsimd.tensor_scalar(neg_shift[:], shift[:], -1.0, 0.0, ALU.mult, ALU.add).then_inc(neg_shift_done, 1)
                pool.wait_ge(neg_shift_done, g.count())
                pool.nop(nofuse=True)
                for c in range(C):
                    last = nc.gpsimd.tensor_scalar(result[:, c, :], h[:, c, :], rstd[i][:, c:c + 1], neg_shift[:, c:c + 1],
                                                   ALU.mult, ALU.add)
                last.then_inc(signal, 1)

            def step(t):
                front, mid, tail = t + 2, t + 1, t + (-1)

                def front_x_plus():
                    pool.wait_ge(x_landed[front.parity], front.count_of_parity())
                    if mid.started:
                        pool.wait_ge(h0_done, mid.count(C))
                    for c in range(C):
                        last = nc.gpsimd.tensor_tensor(x_plus[:, c, :], x_sb[front.parity][:, c, :], bv0_row[:], ALU.add)
                    last.then_inc(x_plus_done, 1)

                def tail_rsum_wide():
                    pool.wait_ge(rsum_done, tail.count())
                    if (tail + (-1)).started:
                        pool.wait_ge(r_full, (tail + (-1)).count())
                    pool.nop(nofuse=True)
                    nc.gpsimd.tensor_scalar(rsum_wide[:].rearrange("p c (h d) -> p (c h) d", d=HD),
                                            rsum[:].rearrange("p c h -> p (c h)").unsqueeze(2).to_broadcast([P, C * HEADS, HD]),
                                            1.0, 0.0, ALU.mult, ALU.add).then_inc(rsum_wide_done, 1)

                def heads_x1_plus():
                    if t.peeled and t.offset == 0:
                        pool.wait_ge(setup_copied, len(SETUP))
                    pool.wait_ge(x1_done, t.count())
                    if (t + (-2)).started:
                        pool.wait_ge(h1_done, (t + (-2)).count(C))
                    for c in range(C):
                        last = nc.gpsimd.tensor_tensor(x1_plus[t.parity][:, c, :], x1[t.parity][:, c, :], out_bias[:], ALU.add)
                    last.then_inc(x1_plus_done, 1)

                def tail_normalise():
                    if (tail + (-2)).started:
                        pool.wait_ge(out_stored[tail.parity], (tail + (-2)).count_of_parity())
                    normalise(1, tail, h1, out_sb[tail.parity], out_done)

                stages = {"rstd0": (mid, lambda: inverse_deviation(0, mid)), "x_plus": (front, front_x_plus),
                          "rsum_wide": (tail, tail_rsum_wide), "x1_plus": (t, heads_x1_plus),
                          "rstd1": (tail, lambda: inverse_deviation(1, tail)), "norm1": (tail, tail_normalise)}
                for name in GPSIMD_ORDER.split():
                    if stages[name][0].valid:
                        stages[name][1]()

            pipeline(pool, step)

        @block.tensor
        def _(pe):
            def three_passes(dst, lhs, rhs, lhs_cols, rhs_cols=slice(0, D)):
                terms = [(lhs[a][:, k, lhs_cols], rhs[b][:, k, rhs_cols]) for k in range(C) for a, b in ((0, 0), (0, 1), (1, 0))]
                for n, (left, right) in enumerate(terms):
                    mm = nc.tensor.matmul(dst, left, right, start=(n == 0), stop=(n == len(terms) - 1))
                return mm

            def transposes(dst, src):
                for a in range(C):
                    for c in range(C):
                        mm = nc.tensor.transpose(dst[:, a, c * P:(c + 1) * P], src[:, c, a * P:(a + 1) * P], ident[:])
                return mm

            pe.wait_ge(consts_made, 2)
            pe.wait_ge(weights_landed, 16 * SETUP_LOADS)
            for i, name in enumerate(SETUP):
                ps = work[i % len(work)]
                if i >= 3:
                    pe.wait_ge(setup_copied, i - 2)
                if name == "m0":
                    for a in range(C):
                        for k in range(C):
                            mm = nc.tensor.matmul(ps[:, a, :], natural["wq0"][:, k, a * P:(a + 1) * P], natural["wk0"][:, k, :],
                                                  start=(k == 0), stop=(k == C - 1))
                elif name == "cols":
                    for a in range(C):
                        for k in range(C):
                            nc.tensor.matmul(ps[:, 0, a:a + 1], natural["wk0"][:, k, a * P:(a + 1) * P], bq0_col[:, k:k + 1],
                                             start=(k == 0), stop=(k == C - 1))
                    for k in range(C):
                        mm = nc.tensor.matmul(ps[:, 0, C:C + 1], bq0_col[:, k:k + 1].to_broadcast([P, P]), bk0_col[:, k:k + 1],
                                              start=(k == 0), stop=(k == C - 1))
                elif name == "rows":
                    for k in range(C):
                        mm = nc.tensor.matmul(ps[:, 0, :], bk0_col[:, k:k + 1].to_broadcast([P, P]), natural["wq0"][:, k, :],
                                              start=(k == 0), stop=(k == C - 1))
                elif name == "out_bias":
                    pe.wait_ge(setup_copied, SETUP.index("wo1") + 1)
                    for k in range(C):
                        mm = nc.tensor.matmul(ps[:, 0, :], bv1_col[:, k:k + 1].to_broadcast([P, P]), woT[:, k, :],
                                              start=(k == 0), stop=(k == C - 1))
                else:
                    mm = transposes(ps, natural[name])
                mm.then_inc(setup_ps_full, 1)
            pe.wait_ge(setup_copied, len(SETUP))

            def transpose_head(g, h):
                pe.wait_ge(probs_done, g.count(HEADS * C, (h + 1) * C))
                before, hb = (g, h - 2) if h >= 2 else (g + (-1), h + HEADS - 2)
                if before.started:
                    if hb in ACT_PT:
                        pe.wait_ge(pT_by_act, before.count(n_act, act_pt_before[hb + 1]))
                    else:
                        pe.wait_ge(pT_by_dve, before.count(n_dve, hb + 1 - act_pt_before[hb + 1]))
                transposes(pT_ps[h % 2], probs[h % RING]).then_inc(pT_full, 1)

            def attend(g, group):
                last = (group + 1) * PER_GROUP
                pe.wait_ge(pT_by_act, g.count(n_act, act_pt_before[last]))
                if last > act_pt_before[last]:
                    pe.wait_ge(pT_by_dve, g.count(n_dve, last - act_pt_before[last]))
                if group == 0:
                    pe.wait_ge(v1_done, g.count())
                    if (g + (-1)).started:
                        pe.wait_ge(oT_done, (g + (-1)).count())
                for k in range(C):
                    for r in range(PER_GROUP):
                        h = group * PER_GROUP + r
                        mm = nc.tensor.matmul(oT_ps[HD * r:HD * r + HD, group, :], v1_sb[g.parity][:, k, h * HD:(h + 1) * HD],
                                              pT_sb[h][:, k, :], start=(k == 0), stop=(k == C - 1), tile_position=(0, HD * r))
                mm.then_inc(oT_full, 1)

            def step(t):
                coming, front, mid, tail = t + 3, t + 2, t + 1, t + (-1)

                def scores(s):
                    if s % 2 == 0:
                        pe.wait_ge(stacked[t.parity][s // 2], t.count_of_parity(4 * 16))
                    before, hb = (t, s - 2) if s >= 2 else (t + (-1), s + HEADS - 2)
                    if before.started:
                        pe.wait_ge(masked_done, before.count(HEADS * C, (hb + 1) * C))
                    for c in range(C):
                        mm = nc.tensor.matmul(score_ps[s % 2][:, c, :], stacks[t.parity][:, 0, s, c * P:(c + 1) * P],
                                              stacks[t.parity][:, 1, s, :], start=True, stop=True)
                    mm.then_inc(score_full, 1)

                def coming_xT():
                    pe.wait_ge(x_landed[coming.parity], coming.count_of_parity())
                    if front.started:
                        pe.wait_ge(v0_done, front.count())
                    transposes(xT_ps, x_sb[coming.parity]).then_inc(xT_full, 1)

                def front_g():
                    pe.wait_ge(xT_lo_done, front.count())
                    for a in range(C):
                        mm = three_passes(g_ps[:, a, :], (w_hi["m0"], w_lo["m0"]), (xT_hi, xT_lo), slice(a * P, (a + 1) * P))
                    mm.then_inc(g_full, 1)

                def mid_x1T():
                    pe.wait_ge(x1_done, mid.count())
                    transposes(x1T_ps, x1[mid.parity]).then_inc(x1T_full, 1)

                def front_v0():
                    pe.wait_ge(xT_lo_done, front.count())
                    if mid.started:
                        pe.wait_ge(q_lo_done, mid.count(C))
                    for a in range(C):
                        mm = three_passes(v0_ps[:, a, :], (xT_hi, xT_lo), (w_hi["wv0"], w_lo["wv0"]), slice(a * P, (a + 1) * P))
                    mm.then_inc(v0_full, 1)

                def mid_q():
                    pe.wait_ge(x1T_lo_done, mid.count())
                    pe.wait_ge(g_lo_done, front.count(C))
                    for a in range(C):
                        mm = three_passes(q_ps[:, a, :], (w_hi["wq1"], w_lo["wq1"]), (x1T_hi, x1T_lo), slice(a * P, (a + 1) * P))
                    mm.then_inc(q_full, 1)

                def front_s0():
                    pe.wait_ge(g_lo_done, front.count(C))
                    if mid.started:
                        pe.wait_ge(x1T_lo_done, mid.count())
                    for c in range(C):
                        mm = three_passes(s0_ps[:, c, :], (g_hi, g_lo), (xT_hi, xT_lo), slice(c * P, (c + 1) * P))
                    mm.then_inc(s0_full, 1)

                def mid_k():
                    if tail.started:
                        pe.wait_ge(r_done, tail.count())
                    for a in range(C):
                        mm = three_passes(k_ps[:, a, :], (w_hi["wk1"], w_lo["wk1"]), (x1T_hi, x1T_lo), slice(a * P, (a + 1) * P))
                    mm.then_inc(k_full, 1)

                def tail_r():
                    pe.wait_ge(rsum_wide_done, tail.count())
                    pe.wait_ge(v1_done, t.count())
                    for gr in range(GROUPS):
                        for c in range(C):
                            mm = nc.tensor.transpose(
                                r_ps[:, gr, c * P:(c + 1) * P],
                                rsum_wide[:, c, gr * P:(gr + 1) * P], ident[:])
                    mm.then_inc(r_full, 1)

                def heads_v1():
                    pe.wait_ge(p0T_done, mid.count())
                    for a in range(C):
                        mm = three_passes(v1_ps[:, a, :], (x1T_hi, x1T_lo), (w_hi["wv1"], w_lo["wv1"]), slice(a * P, (a + 1) * P))
                    mm.then_inc(v1_full, 1)

                def front_p0T():
                    pe.wait_ge(p0m_done, front.count(C))
                    if mid.started:
                        pe.wait_ge(k_lo_done, mid.count(C))
                    transposes(p0T_ps, p0m).then_inc(p0T_full, 1)

                def tail_y():
                    pe.wait_ge(oT_done, tail.count())
                    pe.wait_ge(p0_done, front.count(C))
                    for c in range(C):
                        for k in range(C):
                            mm = nc.tensor.matmul(y_ps[:, c, :], oT_sb[:, k, c * P:(c + 1) * P], woT[:, k, :],
                                                  start=(k == 0), stop=(k == C - 1))
                    mm.then_inc(y_full, 1)

                def front_a0():
                    pe.wait_ge(p0T_done, front.count())
                    if tail.started:
                        pe.wait_ge(h1_done, tail.count(C))
                    for c in range(C):
                        for k in range(C):
                            mm = nc.tensor.matmul(a0_ps[:, c, :], p0T_sb[:, k, c * P:(c + 1) * P], v0_sb[:, k, :],
                                                  start=(k == 0), stop=(k == C - 1))
                    mm.then_inc(a0_full, 1)

                stages = {"v1": (t, heads_v1), "g": (front, front_g), "x1T": (mid, mid_x1T), "r": (tail, tail_r), "q": (mid, mid_q),
                          "s0": (front, front_s0), "k": (mid, mid_k), "v0": (front, front_v0), "y": (tail, tail_y),
                          "p0T": (front, front_p0T), "xT": (coming, coming_xT), "a0": (front, front_a0),
                          "attend_first": (t, lambda: attend(t, 0)), "attend_last": (tail, lambda: attend(tail, 1))}
                for item in TENSOR_ORDER.split():
                    name, _, n = item.partition(":")
                    if name == "scores":
                        if t.valid:
                            scores(int(n))
                    elif name == "transpose":
                        g, h = lagging(t, int(n))
                        if g.valid:
                            transpose_head(g, h)
                    elif stages[name][0].valid:
                        stages[name][1]()

            pipeline(pe, step)

        @block.scalar
        def _(act):
            for i, name in enumerate(split_names):
                act.wait_ge(setup_ps_full, i + 1)
                for a in range(C):
                    last = nc.scalar.copy(by_parts(name, w_hi[name][:, a, :]), by_heads(name, work[i % len(work)][:, a, :]))
                last.then_inc(setup_hi, 1)
            act.wait_ge(setup_copied, len(SETUP))

            def head_exp(g, h):
                for c in range(C):
                    act.wait_ge(neg_max_done, g.count(HEADS, h + 1))
                    if c == 0:
                        before, hb = (g, h - RING) if h >= RING else (g + (-1), h + HEADS - RING)
                        if before.started:
                            act.wait_ge(pT_full, before.count(HEADS, hb + 1))
                        if h == 0 and (g + (-2)).started:
                            act.wait_ge(rsum_done, (g + (-2)).count())
                    nc.scalar.activation(probs[h % RING][:, c, :], masked[h % RING][:, c, :], ACT.Exp, bias=neg_max[:, h, c:c + 1],
                                         scale=SCALE, accum_out=row_sum[g.parity][:, c, h:h + 1]).then_inc(probs_done, 1)

            def copy_pT(g, h):
                if h not in ACT_PT:
                    return
                act.wait_ge(pT_full, g.count(HEADS, h + 1))
                nc.scalar.copy(pT_sb[h][:], pT_ps[h % 2][:]).then_inc(pT_by_act, 1)

            def step(t):
                coming, front, mid, tail = t + 3, t + 2, t + 1, t + (-1)

                def coming_xT():
                    act.wait_ge(xT_full, coming.count())
                    nc.scalar.copy(xT_hi[:], xT_ps[:]).then_inc(xT_hi_done, 1)

                def front_g():
                    act.wait_ge(g_full, front.count())
                    for a in range(C):
                        nc.scalar.activation(g_hi[:, a, :], g_ps[:, a, :], ACT.Identity, bias=g_bias[:, a:a + 1]).then_inc(g_hi_done, 1)

                def front_v0():
                    act.wait_ge(v0_full, front.count())
                    nc.scalar.copy(v0_sb[:], v0_ps[:]).then_inc(v0_done, 1)

                def mid_x1T():
                    act.wait_ge(x1T_full, mid.count())
                    nc.scalar.copy(x1T_hi[:], x1T_ps[:]).then_inc(x1T_hi_done, 1)

                def mid_q():
                    act.wait_ge(q_full, mid.count())
                    if (mid + (-1)).started:
                        pm = mid + (-1)
                        for r in range(PER_GROUP):
                            act.wait_ge(stacked[pm.parity][r], pm.count_of_parity(4 * 16))
                    for a in range(C):
                        nc.scalar.activation(q_parts[:, 0, a, :], q_ps[:, a, :], ACT.Identity, bias=bq1_col[:, a:a + 1]).then_inc(q_hi_done, 1)

                def mid_k():
                    act.wait_ge(k_full, mid.count())
                    for a in range(C):
                        nc.scalar.activation(k_parts[:, 0, a, :], k_ps[:, a, :], ACT.Identity, bias=bk1_col[:, a:a + 1]).then_inc(k_hi_done, 1)

                def heads_v1():
                    act.wait_ge(v1_full, t.count())
                    nc.scalar.copy(v1_sb[t.parity][:], v1_ps[:]).then_inc(v1_done, 1)

                def tail_r():
                    act.wait_ge(r_full, tail.count())
                    nc.scalar.copy(r_sb[:], r_ps[:]).then_inc(r_done, 1)

                def front_exp():
                    act.wait_ge(s0_full, front.count())
                    act.wait_ge(row_bias_done, front.count())
                    for c in range(C):
                        nc.scalar.activation(p0[:, c, :], s0_ps[:, c, :], ACT.Exp, bias=row_bias[:, c:c + 1]).then_inc(p0_done, 1)

                def front_p0T():
                    act.wait_ge(p0T_full, front.count())
                    nc.scalar.copy(p0T_sb[:], p0T_ps[:]).then_inc(p0T_done, 1)

                stages = {"v1": (t, heads_v1), "g": (front, front_g), "x1T": (mid, mid_x1T), "r": (tail, tail_r), "q": (mid, mid_q),
                          "p0": (front, front_exp), "k": (mid, mid_k), "v0": (front, front_v0), "p0T": (front, front_p0T),
                          "xT": (coming, coming_xT)}
                for item in SCALAR_ORDER.split():
                    name, _, n = item.partition(":")
                    if name == "exp":
                        if t.valid:
                            head_exp(t, int(n))
                    elif name == "copy":
                        g, h = lagging(t, int(n))
                        if g.valid:
                            copy_pT(g, h)
                    elif stages[name][0].valid:
                        stages[name][1]()

            pipeline(act, step)

        @block.vector
        def _(dve):
            dve.wait_ge(weights_landed, 16 * SETUP_LOADS)
            for i, name in enumerate(SETUP):
                ps = work[i % len(work)]
                dve.wait_ge(setup_ps_full, i + 1)
                if name in split_names:
                    dve.wait_ge(setup_hi, i + 1)
                    for a in range(C):
                        last = nc.vector.tensor_tensor(by_parts(name, w_lo[name][:, a, :]), by_heads(name, ps[:, a, :]),
                                                       by_parts(name, f32(w_hi[name][:, a, :])), ALU.subtract)
                elif name == "wo1":
                    last = nc.vector.tensor_copy(woT[:], ps[:])
                elif name == "cols":
                    nc.vector.tensor_copy(g_bias[:], ps[:, 0, 0:C])
                    last = nc.vector.tensor_copy(key_const[:], ps[:, 0, C:C + 1])
                elif name == "rows":
                    last = nc.vector.tensor_copy(key_row[:], ps[:, 0, :])
                else:
                    last = nc.vector.tensor_tensor(out_bias[:], ps[:, 0, :], bo1_row[:], ALU.add)
                last.then_inc(setup_copied, 1)
            dve.wait_ge(setup_copied, len(SETUP))

            def lo_part(lo, ps, hi, bias=None):
                if bias is None:
                    return [nc.vector.tensor_tensor(lo, ps, f32(hi), ALU.subtract)]
                return [nc.vector.scalar_tensor_tensor(out=lo[:, a, :], in0=ps[:, a, :], scalar=bias[:, a:a + 1], in1=f32(hi[:, a, :]),
                                                       op0=ALU.add, op1=ALU.subtract) for a in range(C)]

            def head_mask(g, h):
                dve.wait_ge(score_full, g.count(HEADS, h + 1))
                if h == 0:
                    dve.wait_ge(adjh_landed[g.parity], g.count_of_parity())
                before, hb = (g, h - RING) if h >= RING else (g + (-1), h + HEADS - RING)
                if before.started:
                    dve.wait_ge(probs_done, before.count(HEADS * C, (hb + 1) * C))
                dve.nop(nofuse=True)
                for c in range(C):
                    nc.vector.tensor_tensor_reduce(masked[h % RING][:, c, :], score_ps[h % 2][:, c, :], adj_heads[g.parity][:, c, :],
                                                   1.0, LOWEST, ALU.mult, ALU.max, row_max[:, h, c:c + 1]).then_inc(masked_done, 1)
                dve.wait_ge(masked_done, g.count(HEADS * C, (h + 1) * C))
                nc.vector.tensor_scalar(neg_max[:, h, :], row_max[:, h, :], -SCALE, None, ALU.mult).then_inc(neg_max_done, 1)

            def copy_pT(g, h):
                if h in ACT_PT:
                    return
                dve.wait_ge(pT_full, g.count(HEADS, h + 1))
                nc.vector.tensor_copy(pT_sb[h][:], pT_ps[h % 2][:]).then_inc(pT_by_dve, 1)

            def residual(g, h, ps, scale, plus, signal, norm_done):
                if (g + (-1)).started:
                    dve.wait_ge(norm_done, (g + (-1)).count())
                for c in range(C):
                    if scale is None:
                        nc.vector.tensor_tensor(h[:, c, :], ps[:, c, :], plus[:, c, :], ALU.add).then_inc(signal, 1)
                    else:
                        nc.vector.scalar_tensor_tensor(out=h[:, c, :], in0=ps[:, c, :], scalar=scale[:, c:c + 1], in1=plus[:, c, :],
                                                       op0=ALU.mult, op1=ALU.add).then_inc(signal, 1)

            def row_stats(i, g, h, signal):
                for c in range(C):
                    dve.wait_ge(signal, g.count(C, c + 1))
                    nc.vector.bn_stats(stats[i][:, c, :], h[:, c, :]).then_inc(stats_done[i], 1)
                for c in range(C):
                    dve.wait_ge(stats_done[i], g.count(C, c + 1))
                    dve.nop(nofuse=True)
                    nc.vector.bn_aggr(mean_var[i][:, c, :], stats[i][:, c, :]).then_inc(mean_var_done[i], 1)

            def step(t):
                coming, front, mid, tail = t + 3, t + 2, t + 1, t + (-1)

                def coming_xT():
                    dve.wait_ge(xT_hi_done, coming.count())
                    lo_part(xT_lo[:], xT_ps[:], xT_hi[:])[-1].then_inc(xT_lo_done, 1)

                def tail_rsum():
                    dve.wait_ge(probs_done, tail.count(HEADS * C))
                    nc.vector.reciprocal(rsum[:], row_sum[tail.parity][:]).then_inc(rsum_done, 1)

                def front_g():
                    dve.wait_ge(g_hi_done, front.count(C))
                    for op in lo_part(g_lo, g_ps, g_hi, g_bias):
                        op.then_inc(g_lo_done, 1)

                def front_rows():
                    dve.wait_ge(x_landed[front.parity], front.count_of_parity())
                    if (front + (-1)).started:
                        dve.wait_ge(row_bias_done, (front + (-1)).count())
                    for c in range(C):
                        nc.vector.tensor_tensor_reduce(scratch[:, c, :], x_sb[front.parity][:, c, :], key_row[:], 1.0, 0.0,
                                                       ALU.mult, ALU.add, row_dot[:, c:c + 1]).then_inc(row_dot_done, 1)
                    dve.wait_ge(row_dot_done, front.count(C))
                    if (front + (-1)).started:
                        dve.wait_ge(p0_done, (front + (-1)).count(C))
                    nc.vector.tensor_scalar(row_bias[:], row_dot[:], key_const[:, 0:1], None, ALU.add).then_inc(row_bias_done, 1)

                def mid_x1T():
                    dve.wait_ge(x1T_hi_done, mid.count())
                    lo_part(x1T_lo[:], x1T_ps[:], x1T_hi[:])[-1].then_inc(x1T_lo_done, 1)

                def tail_oT():
                    dve.wait_ge(r_done, tail.count())
                    dve.wait_ge(oT_full, tail.count(GROUPS))
                    nc.vector.tensor_tensor(oT_sb[:], oT_ps[:], r_sb[:], ALU.mult).then_inc(oT_done, 1)

                def front_mask():
                    dve.wait_ge(adjf_landed[front.parity], front.count_of_parity())
                    for c in range(C):
                        dve.wait_ge(p0_done, front.count(C, c + 1))
                        nc.vector.tensor_tensor_reduce(p0m[:, c, :], p0[:, c, :], adj_front[front.parity][:, c, :], 1.0, 0.0,
                                                       ALU.mult, ALU.add, sum0[:, c:c + 1]).then_inc(p0m_done, 1)
                    dve.wait_ge(p0m_done, front.count(C))
                    nc.vector.reciprocal(rsum0[:], sum0[:]).then_inc(rsum0_done, 1)

                def mid_q():
                    dve.wait_ge(q_hi_done, mid.count(C))
                    for op in lo_part(q_parts[:, 1], q_ps, q_parts[:, 0], bq1_col):
                        op.then_inc(q_lo_done, 1)

                def mid_k():
                    dve.wait_ge(k_hi_done, mid.count(C))
                    for op in lo_part(k_parts[:, 1], k_ps, k_parts[:, 0], bk1_col):
                        op.then_inc(k_lo_done, 1)

                def tail_h1():
                    dve.wait_ge(y_full, tail.count())
                    dve.wait_ge(x1_plus_done, tail.count())
                    residual(tail, h1, y_ps, None, x1_plus[tail.parity], h1_done, out_done)

                def tail_stats():
                    row_stats(1, tail, h1, h1_done)

                def front_h0():
                    dve.wait_ge(a0_full, front.count())
                    dve.wait_ge(x_plus_done, front.count())
                    dve.wait_ge(rsum0_done, front.count())
                    residual(front, h0, a0_ps, rsum0, x_plus, h0_done, x1_done)

                def mid_stats():
                    row_stats(0, mid, h0, h0_done)

                def mid_norm():
                    dve.wait_ge(rstd_done[0], mid.count())
                    if (mid + (-2)).started:
                        dve.wait_ge(x1_plus_done, (mid + (-2)).count())
                        dve.wait_ge(x1T_full, (mid + (-2)).count())
                    for c in range(C):
                        last = nc.vector.tensor_scalar(x1[mid.parity][:, c, :], h0[:, c, :], mean_var[0][:, c, 0:1], rstd[0][:, c:c + 1],
                                                       ALU.subtract, ALU.mult)
                    last.then_inc(x1_done, 1)

                stages = {"stats0": (mid, mid_stats), "rsum": (tail, tail_rsum), "norm0": (mid, mid_norm), "g": (front, front_g),
                          "x1T": (mid, mid_x1T), "rows": (front, front_rows), "q": (mid, mid_q), "oT": (tail, tail_oT),
                          "p0m": (front, front_mask), "k": (mid, mid_k), "h1": (tail, tail_h1), "stats1": (tail, tail_stats),
                          "xT": (coming, coming_xT), "h0": (front, front_h0)}
                for item in VECTOR_ORDER.split():
                    name, _, n = item.partition(":")
                    if name == "mask":
                        if t.valid:
                            head_mask(t, int(n))
                    elif name == "copy":
                        g, h = lagging(t, int(n))
                        if g.valid:
                            copy_pT(g, h)
                    elif stages[name][0].valid:
                        stages[name][1]()

            pipeline(dve, step)


INPUTS = ["x", "adj", "L0_gnn_Wq_w", "L0_gnn_Wq_b", "L0_gnn_Wk_w", "L0_gnn_Wk_b", "L0_gnn_Wv_w", "L0_gnn_Wv_b",
          "L1_gnn_Wq", "L1_gnn_bq", "L1_gnn_Wk", "L1_gnn_bk", "L1_gnn_Wv", "L1_gnn_bv", "L1_gnn_Wo", "L1_gnn_bo"]


def kernel(**inputs):
    import numpy as np
    import concourse.bacc as bacc
    from concourse.bass_utils import run_bass_kernel_spmd

    nc = bacc.Bacc("TRN2", target_bir_lowering=False, num_devices=1)
    arrays, args = {}, []
    for name in INPUTS:
        a = np.ascontiguousarray(inputs[name])
        arrays[f"in_{name}"] = a
        args.append(nc.dram_tensor(f"in_{name}", a.shape, mybir.dt.from_np(a.dtype), kind="ExternalInput").ap())
    out = nc.dram_tensor("out_x", (B, N, D), F32, kind="ExternalOutput").ap()
    build(nc, *args, out)
    r = run_bass_kernel_spmd(nc, [arrays], core_ids=[0])
    return r.results[0]["out_x"]
```

```python
from contextlib import ExitStack

import concourse.bass as bass
from concourse import mybir

F32 = mybir.dt.float32
F32R = mybir.dt.float32r
ALU = mybir.AluOpType
ACT = mybir.ActivationFunctionType

P = 128
B = 32
N = 256
D = 256
C = N // P
HEADS = 8
HD = D // HEADS
GROUPS = 2
PER_GROUP = HEADS // GROUPS
SCALE = 2.0 * float(HD) ** -0.5
EPS = 1e-5
LOWEST = -3.0e38
LAG = 2
RING = 4
ACT_PT = (1, 2, 4, 5, 6, 7,)

TENSOR_ORDER = """
transpose:0 scores:0 v1

scores:1 transpose:1 g scores:2 x1T attend_last transpose:2
r scores:3 q scores:4 transpose:3 s0 scores:5 k

transpose:4
v0 scores:6 transpose:5 p0T scores:7 y attend_first
xT transpose:6 transpose:7 a0
"""
SCALAR_ORDER = """
v1
copy:0 exp:0 g copy:1
x1T exp:1 exp:2 q copy:2
r copy:3 exp:3 oT p0
k
copy:4 v0 exp:4 copy:5 exp:5
p0T xT exp:6 copy:6
copy:7 exp:7
"""
VECTOR_ORDER = """
copy:0 mask:0
stats0 mask:1 norm0 rsum g x1T mask:2 rows copy:1

mask:3 q oT copy:2 copy:3 mask:4 p0m
copy:4 k
mask:5 copy:5
v0 copy:6 mask:6 p0T h1 stats1 mask:7 xT
copy:7 h0
"""
GPSIMD_ORDER = """
rstd0 x1_plus rsum_wide x_plus oT_lo rstd1 norm1
"""

SETUP = ("m0", "biases", "wv0", "wq1", "wk1", "wv1", "wo1", "out_bias")
SPLIT = tuple(name for name in SETUP if name not in ("biases", "out_bias"))
TENSOR_FILL = {
    -3: "xT setup:m0 setup:biases",
    -2: "g setup:wv0 s0 v0 setup:wq1 p0T xT a0",
    -1: "g setup:wk1 x1T setup:wv1 setup:wo1 q s0 k v0 setup:out_bias p0T xT a0",
}
SCALAR_FILL = {
    -3: "xT setup:m0",
    -2: "g setup:wv0 p0 v0 p0T setup:wq1 xT",
    -1: "g setup:wk1 x1T setup:wv1 q setup:wo1 p0 k v0 p0T xT",
}
VECTOR_FILL = {
    -3: "xT setup:m0 setup:biases",
    -2: "g setup:wv0 rows p0m v0 p0T setup:wq1 xT h0",
    -1: "stats0 norm0 g setup:wk1 x1T rows setup:wv1 q setup:wo1 p0m k v0 p0T setup:out_bias xT h0",
}


class Graph:

    def __init__(self, loop, offset):
        self.loop, self.offset = loop, offset
        self.parity = offset % 2
        self.peeled = isinstance(loop, int)

    def __add__(self, k):
        return Graph(self.loop, self.offset + k)

    @property
    def valid(self):
        return not self.peeled or 0 <= self.offset < B

    @property
    def index(self):
        return self.offset if self.peeled else self.loop * 2 + self.offset

    def count(self, n=1, k=None):
        k = n if k is None else k
        if self.peeled:
            return self.offset * n + k if self.offset < B else B * n
        return self.loop * (2 * n) + (self.offset * n + k)

    def count_of_parity(self, n=16):
        if self.peeled:
            return (self.offset // 2 + 1) * n
        return self.loop * n + (self.offset // 2 + 1) * n

    @property
    def started(self):
        return not self.peeled or self.offset >= 0


def build(nc, x, adj, wq0, bq0, wk0, bk0, wv0, bv0, wq1, bq1, wk1, bk1, wv1, bv1, wo1, bo1, out):
    ctx = ExitStack()
    with ctx:
        def sb(name, shape, dt=F32):
            return ctx.enter_context(nc.sbuf_tensor(name, [P, *shape], dt))

        def sem(name):
            return ctx.enter_context(nc.semaphore(name))

        weights = {"wq0": wq0, "wk0": wk0, "wv0": wv0, "wq1": wq1, "wk1": wk1, "wv1": wv1, "wo1": wo1}
        natural = {n: sb(n + "_sb", [C, D]) for n in weights}
        w_hi = {n: sb(n + "_hi", [C, D], F32R) for n in SPLIT}
        w_lo = {n: sb(n + "_lo", [C, D], F32R) for n in SPLIT}
        woT = sb("woT", [C, D])
        ident = sb("ident", [P])
        bq0_col, bk0_col, bq1_col, bk1_col, bv1_col = (sb(n, [C]) for n in ("bq0_col", "bk0_col", "bq1_col", "bk1_col", "bv1_col"))
        bv0_row, bo1_row = sb("bv0_row", [D]), sb("bo1_row", [D])
        out_bias = sb("out_bias", [D])
        g_bias = sb("g_bias", [C])
        key_row = sb("key_row", [D])
        key_const = sb("key_const", [1])
        minus_half = sb("minus_half", [C])

        x_sb = [sb(f"x{i}", [C, D]) for i in range(2)]
        adj_front = [sb(f"adj_front{i}", [C, N]) for i in range(2)]
        x_plus = sb("x_plus", [C, D])
        xT_hi, xT_lo = sb("xT_hi", [C, N], F32R), sb("xT_lo", [C, N], F32R)
        g_hi, g_lo = sb("g_hi", [C, N], F32R), sb("g_lo", [C, N], F32R)
        v0_hi, v0_lo = sb("v0_hi", [C, D], F32R), sb("v0_lo", [C, D], F32R)
        row_dot = sb("row_dot", [C])
        row_bias = sb("row_bias", [C])
        scratch = sb("scratch", [C, D])
        p0 = sb("p0", [C, N])
        p0m = sb("p0m", [C, N])
        sum0, rsum0 = sb("sum0", [C]), sb("rsum0", [C])
        p0T_hi, p0T_lo = sb("p0T_hi", [C, N], F32R), sb("p0T_lo", [C, N], F32R)
        h0 = sb("h0", [C, D])
        x1 = [sb(f"x1_{i}", [C, D]) for i in range(2)]
        x1T_hi, x1T_lo = sb("x1T_hi", [C, N], F32R), sb("x1T_lo", [C, N], F32R)
        parts = sb("parts", [4, GROUPS, N], F32R)
        q_parts, k_parts = parts[:, 0:2], parts[:, 2:4]
        stacks = [sb(f"stacks{i}", [2, HEADS, N], F32R) for i in range(2)]
        v1_sb = [sb(f"v1_{i}", [C, D]) for i in range(2)]
        adj_heads = [sb(f"adj_heads{i}", [C, N]) for i in range(2)]
        masked = [sb(f"masked{i}", [C, N]) for i in range(RING)]
        probs = [sb(f"probs{i}", [C, N]) for i in range(RING)]
        pT_sb = [sb(f"pT{h}", [C, N]) for h in range(HEADS)]
        row_max = sb("row_max", [HEADS, C])
        neg_max = sb("neg_max", [HEADS, C])
        row_sum = [sb(f"row_sum{i}", [C, HEADS]) for i in range(2)]
        rsum = sb("rsum", [C, HEADS])
        rsum_wide = sb("rsum_wide", [C, D])
        r_sb = sb("r_sb", [GROUPS, N])
        oT_sb = sb("oT_sb", [GROUPS, N])
        oT_hi, oT_lo = sb("oT_hi", [GROUPS, N], F32R), sb("oT_lo", [GROUPS, N], F32R)
        x1_plus = [sb(f"x1_plus{i}", [C, D]) for i in range(2)]
        h1 = sb("h1", [C, D])
        out_sb = [sb(f"out{i}", [C, D]) for i in range(2)]
        stats = [sb(f"stats{i}", [C, 6]) for i in range(2)]
        mean_var = [sb(f"mean_var{i}", [C, 2]) for i in range(2)]
        var_eps, rstd = ([sb(f"{n}{i}", [C]) for i in range(2)] for n in ("var_eps", "rstd"))
        shift, neg_shift = sb("shift", [C]), sb("neg_shift", [C])

        def bank(name):
            return ctx.enter_context(nc.psum_tensor(name, [P, 2, 256], F32))

        score_ps = [bank(f"score_ps{i}") for i in range(2)]
        pT_ps = [bank(f"pT_ps{i}") for i in range(2)]
        oT_ps = bank("oT_ps")
        work = [bank(f"work{i}") for i in range(3)]
        v1_ps, r_ps, k_ps, p0T_ps = [work[0]] * 4
        g_ps, q_ps, v0_ps, xT_ps = [work[1]] * 4
        x1T_ps, s0_ps, y_ps, a0_ps = [work[2]] * 4

        x_landed, adjf_landed, adjh_landed = ([sem(f"{n}{i}") for i in range(2)] for n in ("x_landed", "adjf_landed", "adjh_landed"))
        stacked = [[sem(f"stacked{i}_{r}") for r in range(PER_GROUP)] for i in range(2)]
        out_stored = [sem(f"out_stored{i}") for i in range(2)]
        folded_landed, bias0_landed, value_landed, qk_landed, layer1_landed = (
            sem(n + "_landed") for n in ("folded", "bias0", "value", "qk", "layer1"))
        ident_zero, consts_made = sem("ident_zero"), sem("consts_made")
        setup_ps_full, setup_hi, setup_copied = sem("setup_ps_full"), sem("setup_hi"), sem("setup_copied")
        xT_full, g_full, v0_full, s0_full, p0T_full, a0_full = (sem(n + "_full") for n in ("xT", "g", "v0", "s0", "p0T", "a0"))
        x1T_full, q_full, k_full, v1_full = (sem(n + "_full") for n in ("x1T", "q", "k", "v1"))
        score_full, pT_full, oT_full, r_full, y_full = (sem(n + "_full") for n in ("score", "pT", "oT", "r", "y"))
        xT_hi_done, xT_lo_done, g_hi_done, g_lo_done, v0_hi_done, v0_lo_done = (
            sem(n + "_done") for n in ("xT_hi", "xT_lo", "g_hi", "g_lo", "v0_hi", "v0_lo"))
        row_dot_done, row_bias_done, p0_done, p0m_done, rsum0_done, p0T_hi_done, p0T_lo_done, h0_done = (
            sem(n + "_done") for n in ("row_dot", "row_bias", "p0", "p0m", "rsum0", "p0T_hi", "p0T_lo", "h0"))
        x_plus_done, x1_done, x1_plus_done = sem("x_plus_done"), sem("x1_done"), sem("x1_plus_done")
        x1T_hi_done, x1T_lo_done, q_hi_done, q_lo_done, k_hi_done, k_lo_done, v1_done = (
            sem(n + "_done") for n in ("x1T_hi", "x1T_lo", "q_hi", "q_lo", "k_hi", "k_lo", "v1"))
        masked_done, neg_max_done, probs_done = sem("masked_done"), sem("neg_max_done"), sem("probs_done")
        pT_by_act, pT_by_dve = sem("pT_by_act"), sem("pT_by_dve")
        rsum_wide_done = sem("rsum_wide_done")
        rsum_done, r_done, oT_done, oT_hi_done, oT_lo_done, h1_done = (
            sem(n + "_done") for n in ("rsum", "r", "oT", "oT_hi", "oT_lo", "h1"))
        stats_done, mean_var_done, var_eps_done, rstd_done = (
            [sem(f"{n}{i}") for i in range(2)] for n in ("stats_done", "mean_var_done", "var_eps_done", "rstd_done"))
        shift_done, neg_shift_done = sem("shift_done"), sem("neg_shift_done")
        out_done = sem("out_done")

        f32 = lambda ap: ap.bitcast(F32)

        by_chunks = lambda w: w.rearrange("(c p) d -> p c d", p=P)

        def by_parts(name, w):
            return w.rearrange("p (g r d) -> p r g d", g=GROUPS, d=HD) if name in ("wq1", "wk1") else w

        def by_heads(name, w):
            return w.rearrange("p (r g d) -> p r g d", g=GROUPS, d=HD) if name in ("wq1", "wk1") else w

        n_act = len(ACT_PT)
        n_dve = HEADS - n_act
        block = ctx.enter_context(nc.Block())

        setup_ps = {"m0": work[0], "biases": work[2], "wv0": score_ps[0], "wq1": score_ps[1], "wk1": pT_ps[0], "wv1": pT_ps[1],
                    "wo1": oT_ps, "out_bias": score_ps[0]}

        def order_of(t, steady, fill={}):
            return (fill.get(t.offset, steady) if t.peeled else steady).split()

        def wait_setup(eng, g, name):
            if g.peeled and g.offset == 0:
                eng.wait_ge(setup_copied, SETUP.index(name) + 1)

        FIRST_LOOPED, PAIRS = 1, (B - 4) // 2

        def pipeline(eng, step):
            for t in range(-3, FIRST_LOOPED):
                step(Graph(0, t))
            with eng.Fori(0, PAIRS) as loop:
                for u in range(2):
                    step(Graph(loop, FIRST_LOOPED + u))
            for t in range(FIRST_LOOPED + 2 * PAIRS, B + 1):
                step(Graph(0, t))

        def lagging(t, n):
            return (t, n - LAG) if n >= LAG else (t + (-1), n + HEADS - LAG)

        LAYER1_LOADS = 4 + 2 * PER_GROUP
        act_pt_before = [sum(1 for a in ACT_PT if a < h) for h in range(HEADS + 1)]

        @block.sync
        def _(sp):
            def load_x(g):
                sp.dma_start(x_sb[g.parity][:], x[g.index].rearrange("(c p) d -> p c d", p=P)).then_inc(x_landed[g.parity], 16)

            def load_adj(g, tiles, landed):
                sp.dma_start(tiles[g.parity][:], adj[g.index].rearrange("(c p) d -> p c d", p=P)).then_inc(landed[g.parity], 16)

            def load_layer0():
                sp.dma_start(natural["wq0"][:], by_chunks(wq0)).then_inc(folded_landed, 16)
                with nc.allow_non_contiguous_dma(reason="a few hundred bias values, once"):
                    sp.dma_start(bq0_col[:], bq0.rearrange("(c p) -> p c", p=P)).then_inc(bias0_landed, 16)
                    sp.dma_start(bv0_row[:], bv0.rearrange("(a d) -> a d", a=1).to_broadcast([P, D])).then_inc(value_landed, 16)

            def load_layer1():
                for n in ("wq1", "wk1"):
                    sp.dma_start(natural[n][:], by_chunks(weights[n])).then_inc(qk_landed, 16)
                for n in ("wv1", "wo1"):
                    sp.dma_start(natural[n][:], by_chunks(weights[n])).then_inc(layer1_landed, 16)
                with nc.allow_non_contiguous_dma(reason="a few hundred bias values, once"):
                    sp.dma_start(bv1_col[:], bv1.rearrange("(c p) -> p c", p=P)).then_inc(layer1_landed, 16)
                    sp.dma_start(bo1_row[:], bo1.rearrange("(a d) -> a d", a=1).to_broadcast([P, D])).then_inc(layer1_landed, 16)
                    for tile, b in ((bq1_col, bq1), (bk1_col, bk1)):
                        for r in range(PER_GROUP):
                            sp.dma_start(tile[HD * r:HD * r + HD, :], b.rearrange("(r g d) -> r d g", g=GROUPS, d=HD)[r]).then_inc(layer1_landed, 16)

            def stack(g):
                for r in range(PER_GROUP):
                    for c, (q_part, k_part) in enumerate(((0, 2), (1, 3), (0, 3), (1, 2))):
                        sp.dma_start(f32(stacks[g.parity][HD * c:HD * c + HD, :, 2 * r:2 * r + 2, :]),
                                     f32(parts[HD * r:HD * r + HD, q_part:k_part + 1:k_part - q_part, :, :])).then_inc(stacked[g.parity][r], 16)

            def step(t):
                front, mid, tail = t + 2, t + 1, t + (-1)
                nxt = front + 1
                if t.peeled and t.offset == -1:
                    load_layer1()
                if nxt.valid:
                    if (nxt + (-2)).started:
                        sp.wait_ge(xT_full, (nxt + (-2)).count())
                        sp.nop(nofuse=True)
                        sp.wait_ge(row_dot_done, (nxt + (-2)).count(C))
                        sp.wait_ge(x_plus_done, (nxt + (-2)).count())
                    sp.nop(nofuse=True)
                    load_x(nxt)
                    if t.peeled and t.offset == -3:
                        load_layer0()
                    if (nxt + (-2)).started:
                        sp.wait_ge(p0m_done, (nxt + (-2)).count(C))
                    sp.nop(nofuse=True)
                    load_adj(nxt, adj_front, adjf_landed)
                if mid.valid:
                    if (mid + (-2)).started:
                        sp.wait_ge(masked_done, (mid + (-2)).count(HEADS * C))
                    sp.nop(nofuse=True)
                    load_adj(mid, adj_heads, adjh_landed)
                    if (mid + (-2)).started:
                        sp.wait_ge(score_full, (mid + (-2)).count(HEADS))
                    sp.wait_ge(q_lo_done, mid.count(C))
                    sp.wait_ge(k_lo_done, mid.count(C))
                    sp.nop(nofuse=True)
                    stack(mid)
                if tail.valid:
                    sp.wait_ge(out_done, tail.count())
                    sp.nop(nofuse=True)
                    sp.dma_start(out[tail.index].rearrange("(c p) d -> p c d", p=P), out_sb[tail.parity][:]).then_inc(out_stored[tail.parity], 16)

            pipeline(sp, step)
            for i in range(2):
                sp.wait_ge(out_stored[i], 16 * (B // 2))

        @block.gpsimd
        def _(pool):
            nc.gpsimd.memset(ident[:], 0.0).then_inc(ident_zero, 1)
            nc.gpsimd.memset(minus_half[:], -0.5).then_inc(consts_made, 1)
            pool.wait_ge(ident_zero, 1)
            nc.gpsimd.affine_select(out=ident[:], in_=ident[:], compare_op=ALU.not_equal, fill=1.0, base=0,
                                    pattern=[[-1, P]], channel_multiplier=1).then_inc(consts_made, 1)
            pool.wait_ge(consts_made, 2)
            pool.wait_ge(value_landed, 16 * 2)

            def inverse_deviation(i, g):
                pool.wait_ge(mean_var_done[i], g.count(C))
                pool.nop(nofuse=True)
                nc.gpsimd.tensor_scalar(var_eps[i][:], mean_var[i][:, :, 1], 1.0, EPS, ALU.mult, ALU.add).then_inc(var_eps_done[i], 1)
                pool.wait_ge(var_eps_done[i], g.count())
                nc.gpsimd.tensor_tensor(rstd[i][:], var_eps[i][:], minus_half[:], ALU.pow).then_inc(rstd_done[i], 1)

            def normalise(i, g, h, result, signal):
                pool.wait_ge(rstd_done[i], g.count())
                nc.gpsimd.tensor_tensor(shift[:], mean_var[i][:, :, 0], rstd[i][:], ALU.mult).then_inc(shift_done, 1)
                pool.wait_ge(shift_done, g.count())
                pool.nop(nofuse=True)
                nc.gpsimd.tensor_scalar(neg_shift[:], shift[:], -1.0, 0.0, ALU.mult, ALU.add).then_inc(neg_shift_done, 1)
                pool.wait_ge(neg_shift_done, g.count())
                pool.nop(nofuse=True)
                for c in range(C):
                    last = nc.gpsimd.tensor_scalar(result[:, c, :], h[:, c, :], rstd[i][:, c:c + 1], neg_shift[:, c:c + 1],
                                                   ALU.mult, ALU.add)
                last.then_inc(signal, 1)

            def step(t):
                front, mid, tail = t + 2, t + 1, t + (-1)

                def front_x_plus():
                    pool.wait_ge(x_landed[front.parity], front.count_of_parity())
                    if mid.started:
                        pool.wait_ge(h0_done, mid.count(C))
                    for c in range(C):
                        last = nc.gpsimd.tensor_tensor(x_plus[:, c, :], x_sb[front.parity][:, c, :], bv0_row[:], ALU.add)
                    last.then_inc(x_plus_done, 1)

                def tail_rsum_wide():
                    pool.wait_ge(rsum_done, tail.count())
                    if (tail + (-1)).started:
                        pool.wait_ge(r_full, (tail + (-1)).count())
                    pool.nop(nofuse=True)
                    nc.gpsimd.tensor_scalar(rsum_wide[:].rearrange("p c (h d) -> p (c h) d", d=HD),
                                            rsum[:].rearrange("p c h -> p (c h)").unsqueeze(2).to_broadcast([P, C * HEADS, HD]),
                                            1.0, 0.0, ALU.mult, ALU.add).then_inc(rsum_wide_done, 1)

                def tail_oT_lo():
                    pool.wait_ge(oT_hi_done, tail.count())
                    nc.gpsimd.tensor_tensor(oT_lo[:], oT_sb[:], f32(oT_hi[:]), ALU.subtract).then_inc(oT_lo_done, 1)

                def heads_x1_plus():
                    wait_setup(pool, t, "out_bias")
                    pool.wait_ge(x1_done, t.count(C))
                    if (t + (-2)).started:
                        pool.wait_ge(h1_done, (t + (-2)).count(C))
                    for c in range(C):
                        last = nc.gpsimd.tensor_tensor(x1_plus[t.parity][:, c, :], x1[t.parity][:, c, :], out_bias[:], ALU.add)
                    last.then_inc(x1_plus_done, 1)

                def tail_normalise():
                    if (tail + (-2)).started:
                        pool.wait_ge(out_stored[tail.parity], (tail + (-2)).count_of_parity())
                    normalise(1, tail, h1, out_sb[tail.parity], out_done)

                stages = {"rstd0": (mid, lambda: inverse_deviation(0, mid)), "x_plus": (front, front_x_plus),
                          "rsum_wide": (tail, tail_rsum_wide), "oT_lo": (tail, tail_oT_lo), "x1_plus": (t, heads_x1_plus),
                          "rstd1": (tail, lambda: inverse_deviation(1, tail)), "norm1": (tail, tail_normalise)}
                for name in GPSIMD_ORDER.split():
                    if stages[name][0].valid:
                        stages[name][1]()

            pipeline(pool, step)

        @block.tensor
        def _(pe):
            def three_passes(dst, lhs, rhs, lhs_cols, rhs_cols=slice(0, D)):
                terms = [(lhs[a][:, k, lhs_cols], rhs[b][:, k, rhs_cols]) for k in range(C) for a, b in ((0, 0), (0, 1), (1, 0))]
                for n, (left, right) in enumerate(terms):
                    mm = nc.tensor.matmul(dst, left, right, start=(n == 0), stop=(n == len(terms) - 1))
                return mm

            def transposes(dst, src, chunk_ready=None):
                for c in range(C):
                    if chunk_ready is not None:
                        chunk_ready(c)
                    for a in range(C):
                        mm = nc.tensor.transpose(dst[:, a, c * P:(c + 1) * P], src[:, c, a * P:(a + 1) * P], ident[:])
                return mm

            pe.wait_ge(consts_made, 2)

            def setup(name):
                ps = setup_ps[name]
                if name == "m0":
                    pe.wait_ge(folded_landed, 16 * 2)
                    for a in range(C):
                        for k in range(C):
                            mm = nc.tensor.matmul(ps[:, a, :], natural["wq0"][:, k, a * P:(a + 1) * P], natural["wk0"][:, k, :],
                                                  start=(k == 0), stop=(k == C - 1))
                elif name == "biases":
                    pe.wait_ge(bias0_landed, 16 * 2)
                    for a in range(C):
                        for k in range(C):
                            nc.tensor.matmul(ps[:, 0, a:a + 1], natural["wk0"][:, k, a * P:(a + 1) * P], bq0_col[:, k:k + 1],
                                             start=(k == 0), stop=(k == C - 1))
                    for k in range(C):
                        nc.tensor.matmul(ps[:, 0, C:C + 1], bq0_col[:, k:k + 1].to_broadcast([P, P]), bk0_col[:, k:k + 1],
                                         start=(k == 0), stop=(k == C - 1))
                    for k in range(C):
                        mm = nc.tensor.matmul(ps[:, 1, :], bk0_col[:, k:k + 1].to_broadcast([P, P]), natural["wq0"][:, k, :],
                                              start=(k == 0), stop=(k == C - 1))
                elif name == "out_bias":
                    pe.wait_ge(setup_copied, SETUP.index("wo1") + 1)
                    for k in range(C):
                        mm = nc.tensor.matmul(ps[:, 0, :], bv1_col[:, k:k + 1].to_broadcast([P, P]), woT[:, k, :],
                                              start=(k == 0), stop=(k == C - 1))
                else:
                    if name == "wv0":
                        pe.wait_ge(value_landed, 16 * 2)
                    elif name == "wq1":
                        pe.wait_ge(qk_landed, 16 * 2)
                    elif name == "wv1":
                        pe.wait_ge(layer1_landed, 16 * LAYER1_LOADS)
                    mm = transposes(ps, natural[name])
                mm.then_inc(setup_ps_full, 1)

            def transpose_head(g, h):
                before, hb = (g, h - 2) if h >= 2 else (g + (-1), h + HEADS - 2)
                if before.started:
                    if hb in ACT_PT:
                        pe.wait_ge(pT_by_act, before.count(n_act, act_pt_before[hb + 1]))
                    else:
                        pe.wait_ge(pT_by_dve, before.count(n_dve, hb + 1 - act_pt_before[hb + 1]))
                transposes(pT_ps[h % 2], probs[h % RING],
                           lambda c: pe.wait_ge(probs_done, g.count(HEADS * C, h * C + c + 1))).then_inc(pT_full, 1)

            def attend(g, group):
                last = (group + 1) * PER_GROUP
                pe.wait_ge(pT_by_act, g.count(n_act, act_pt_before[last]))
                if last > act_pt_before[last]:
                    pe.wait_ge(pT_by_dve, g.count(n_dve, last - act_pt_before[last]))
                if group == 0:
                    pe.wait_ge(v1_done, g.count())
                    if (g + (-1)).started:
                        pe.wait_ge(oT_done, (g + (-1)).count())
                for k in range(C):
                    for r in range(PER_GROUP):
                        h = group * PER_GROUP + r
                        mm = nc.tensor.matmul(oT_ps[HD * r:HD * r + HD, group, :], v1_sb[g.parity][:, k, h * HD:(h + 1) * HD],
                                              pT_sb[h][:, k, :], start=(k == 0), stop=(k == C - 1), tile_position=(0, HD * r))
                mm.then_inc(oT_full, 1)

            def step(t):
                coming, front, mid, tail = t + 3, t + 2, t + 1, t + (-1)

                def scores(s):
                    if s == 0:
                        wait_setup(pe, t, "out_bias")
                    if s % 2 == 0:
                        pe.wait_ge(stacked[t.parity][s // 2], t.count_of_parity(4 * 16))
                    before, hb = (t, s - 2) if s >= 2 else (t + (-1), s + HEADS - 2)
                    if before.started:
                        pe.wait_ge(masked_done, before.count(HEADS * C, (hb + 1) * C))
                    for c in range(C):
                        mm = nc.tensor.matmul(score_ps[s % 2][:, c, :], stacks[t.parity][:, 0, s, c * P:(c + 1) * P],
                                              stacks[t.parity][:, 1, s, :], start=True, stop=True)
                    mm.then_inc(score_full, 1)

                def coming_xT():
                    pe.wait_ge(x_landed[coming.parity], coming.count_of_parity())
                    if front.started:
                        pe.wait_ge(v0_lo_done, front.count())
                    transposes(xT_ps, x_sb[coming.parity]).then_inc(xT_full, 1)

                def front_g():
                    wait_setup(pe, front, "m0")
                    pe.wait_ge(xT_lo_done, front.count())
                    for a in range(C):
                        mm = three_passes(g_ps[:, a, :], (w_hi["m0"], w_lo["m0"]), (xT_hi, xT_lo), slice(a * P, (a + 1) * P))
                    mm.then_inc(g_full, 1)

                def mid_x1T():
                    transposes(x1T_ps, x1[mid.parity], lambda c: pe.wait_ge(x1_done, mid.count(C, c + 1))).then_inc(x1T_full, 1)

                def front_v0():
                    wait_setup(pe, front, "wv0")
                    pe.wait_ge(xT_lo_done, front.count())
                    if mid.started:
                        pe.wait_ge(q_lo_done, mid.count(C))
                    for a in range(C):
                        mm = three_passes(v0_ps[:, a, :], (xT_hi, xT_lo), (w_hi["wv0"], w_lo["wv0"]), slice(a * P, (a + 1) * P))
                    mm.then_inc(v0_full, 1)

                def mid_q():
                    wait_setup(pe, mid, "wq1")
                    pe.wait_ge(x1T_lo_done, mid.count())
                    pe.wait_ge(g_lo_done, front.count(C))
                    for a in range(C):
                        mm = three_passes(q_ps[:, a, :], (w_hi["wq1"], w_lo["wq1"]), (x1T_hi, x1T_lo), slice(a * P, (a + 1) * P))
                    mm.then_inc(q_full, 1)

                def front_s0():
                    pe.wait_ge(g_lo_done, front.count(C))
                    if mid.started:
                        pe.wait_ge(x1T_lo_done, mid.count())
                    for c in range(C):
                        mm = three_passes(s0_ps[:, c, :], (g_hi, g_lo), (xT_hi, xT_lo), slice(c * P, (c + 1) * P))
                    mm.then_inc(s0_full, 1)

                def mid_k():
                    wait_setup(pe, mid, "wk1")
                    if tail.started:
                        pe.wait_ge(r_done, tail.count())
                    for a in range(C):
                        mm = three_passes(k_ps[:, a, :], (w_hi["wk1"], w_lo["wk1"]), (x1T_hi, x1T_lo), slice(a * P, (a + 1) * P))
                    mm.then_inc(k_full, 1)

                def tail_r():
                    pe.wait_ge(rsum_wide_done, tail.count())
                    pe.wait_ge(v1_done, t.count())
                    for gr in range(GROUPS):
                        for c in range(C):
                            mm = nc.tensor.transpose(
                                r_ps[:, gr, c * P:(c + 1) * P],
                                rsum_wide[:, c, gr * P:(gr + 1) * P], ident[:])
                    mm.then_inc(r_full, 1)

                def heads_v1():
                    wait_setup(pe, t, "wv1")
                    pe.wait_ge(p0T_lo_done, mid.count())
                    for a in range(C):
                        mm = three_passes(v1_ps[:, a, :], (x1T_hi, x1T_lo), (w_hi["wv1"], w_lo["wv1"]), slice(a * P, (a + 1) * P))
                    mm.then_inc(v1_full, 1)

                def front_p0T():
                    if mid.started:
                        pe.wait_ge(k_lo_done, mid.count(C))
                    transposes(p0T_ps, p0m, lambda c: pe.wait_ge(p0m_done, front.count(C, c + 1))).then_inc(p0T_full, 1)

                def tail_y():
                    wait_setup(pe, tail, "wo1")
                    pe.wait_ge(oT_hi_done, tail.count())
                    pe.wait_ge(oT_lo_done, tail.count())
                    pe.wait_ge(p0_done, front.count(C))
                    for c in range(C):
                        mm = three_passes(y_ps[:, c, :], (oT_hi, oT_lo), (w_hi["wo1"], w_lo["wo1"]), slice(c * P, (c + 1) * P))
                    mm.then_inc(y_full, 1)

                def front_a0():
                    pe.wait_ge(v0_lo_done, front.count())
                    pe.wait_ge(p0T_lo_done, front.count())
                    if tail.started:
                        pe.wait_ge(h1_done, tail.count(C))
                    for c in range(C):
                        mm = three_passes(a0_ps[:, c, :], (p0T_hi, p0T_lo), (v0_hi, v0_lo), slice(c * P, (c + 1) * P))
                    mm.then_inc(a0_full, 1)

                stages = {"v1": (t, heads_v1), "g": (front, front_g), "x1T": (mid, mid_x1T), "r": (tail, tail_r), "q": (mid, mid_q),
                          "s0": (front, front_s0), "k": (mid, mid_k), "v0": (front, front_v0), "y": (tail, tail_y),
                          "p0T": (front, front_p0T), "xT": (coming, coming_xT), "a0": (front, front_a0),
                          "attend_first": (t, lambda: attend(t, 0)), "attend_last": (tail, lambda: attend(tail, 1))}
                for item in order_of(t, TENSOR_ORDER, TENSOR_FILL):
                    name, _, n = item.partition(":")
                    if name == "setup":
                        setup(n)
                    elif name == "scores":
                        if t.valid:
                            scores(int(n))
                    elif name == "transpose":
                        g, h = lagging(t, int(n))
                        if g.valid:
                            transpose_head(g, h)
                    elif stages[name][0].valid:
                        stages[name][1]()

            pipeline(pe, step)

        @block.scalar
        def _(act):
            act.dma_start(natural["wk0"][:], by_chunks(wk0)).then_inc(folded_landed, 16)
            with nc.allow_non_contiguous_dma(reason="a few hundred bias values, once"):
                act.dma_start(bk0_col[:], bk0.rearrange("(c p) -> p c", p=P)).then_inc(bias0_landed, 16)
            act.dma_start(natural["wv0"][:], by_chunks(wv0)).then_inc(value_landed, 16)

            def setup(name):
                act.wait_ge(setup_ps_full, SETUP.index(name) + 1)
                for a in range(C):
                    last = nc.scalar.copy(by_parts(name, w_hi[name][:, a, :]), by_heads(name, setup_ps[name][:, a, :]))
                last.then_inc(setup_hi, 1)

            def head_exp(g, h):
                for c in range(C):
                    act.wait_ge(neg_max_done, g.count(HEADS, h + 1))
                    if c == 0:
                        before, hb = (g, h - RING) if h >= RING else (g + (-1), h + HEADS - RING)
                        if before.started:
                            act.wait_ge(pT_full, before.count(HEADS, hb + 1))
                        if h == 0 and (g + (-2)).started:
                            act.wait_ge(rsum_done, (g + (-2)).count())
                    nc.scalar.activation(probs[h % RING][:, c, :], masked[h % RING][:, c, :], ACT.Exp, bias=neg_max[:, h, c:c + 1],
                                         scale=SCALE, accum_out=row_sum[g.parity][:, c, h:h + 1]).then_inc(probs_done, 1)

            def copy_pT(g, h):
                if h not in ACT_PT:
                    return
                act.wait_ge(pT_full, g.count(HEADS, h + 1))
                nc.scalar.copy(pT_sb[h][:], pT_ps[h % 2][:]).then_inc(pT_by_act, 1)

            def step(t):
                coming, front, mid, tail = t + 3, t + 2, t + 1, t + (-1)

                def coming_xT():
                    act.wait_ge(xT_full, coming.count())
                    nc.scalar.copy(xT_hi[:], xT_ps[:]).then_inc(xT_hi_done, 1)

                def front_g():
                    wait_setup(act, front, "biases")
                    act.wait_ge(g_full, front.count())
                    for a in range(C):
                        nc.scalar.activation(g_hi[:, a, :], g_ps[:, a, :], ACT.Identity, bias=g_bias[:, a:a + 1]).then_inc(g_hi_done, 1)

                def front_v0():
                    act.wait_ge(v0_full, front.count())
                    nc.scalar.copy(v0_hi[:], v0_ps[:]).then_inc(v0_hi_done, 1)

                def mid_x1T():
                    act.wait_ge(x1T_full, mid.count())
                    nc.scalar.copy(x1T_hi[:], x1T_ps[:]).then_inc(x1T_hi_done, 1)

                def mid_q():
                    if mid.peeled and mid.offset == 0:
                        act.wait_ge(layer1_landed, 16 * LAYER1_LOADS)
                    if (mid + (-1)).started:
                        pm = mid + (-1)
                        for r in range(PER_GROUP):
                            act.wait_ge(stacked[pm.parity][r], pm.count_of_parity(4 * 16))
                    act.wait_ge(q_full, mid.count())
                    for a in range(C):
                        nc.scalar.activation(q_parts[:, 0, a, :], q_ps[:, a, :], ACT.Identity, bias=bq1_col[:, a:a + 1]).then_inc(q_hi_done, 1)

                def mid_k():
                    act.wait_ge(k_full, mid.count())
                    for a in range(C):
                        nc.scalar.activation(k_parts[:, 0, a, :], k_ps[:, a, :], ACT.Identity, bias=bk1_col[:, a:a + 1]).then_inc(k_hi_done, 1)

                def heads_v1():
                    act.wait_ge(v1_full, t.count())
                    nc.scalar.copy(v1_sb[t.parity][:], v1_ps[:]).then_inc(v1_done, 1)

                def tail_r():
                    act.wait_ge(r_full, tail.count())
                    nc.scalar.copy(r_sb[:], r_ps[:]).then_inc(r_done, 1)

                def front_exp():
                    act.wait_ge(row_bias_done, front.count())
                    act.wait_ge(s0_full, front.count())
                    for c in range(C):
                        nc.scalar.activation(p0[:, c, :], s0_ps[:, c, :], ACT.Exp, bias=row_bias[:, c:c + 1]).then_inc(p0_done, 1)

                def front_p0T():
                    act.wait_ge(p0T_full, front.count())
                    nc.scalar.copy(p0T_hi[:], p0T_ps[:]).then_inc(p0T_hi_done, 1)

                def tail_oT():
                    act.wait_ge(oT_done, tail.count())
                    nc.scalar.copy(oT_hi[:], oT_sb[:]).then_inc(oT_hi_done, 1)

                stages = {"v1": (t, heads_v1), "g": (front, front_g), "x1T": (mid, mid_x1T), "r": (tail, tail_r), "q": (mid, mid_q),
                          "p0": (front, front_exp), "k": (mid, mid_k), "v0": (front, front_v0), "p0T": (front, front_p0T),
                          "oT": (tail, tail_oT), "xT": (coming, coming_xT)}
                for item in order_of(t, SCALAR_ORDER, SCALAR_FILL):
                    name, _, n = item.partition(":")
                    if name == "setup":
                        setup(n)
                    elif name == "exp":
                        if t.valid:
                            head_exp(t, int(n))
                    elif name == "copy":
                        g, h = lagging(t, int(n))
                        if g.valid:
                            copy_pT(g, h)
                    elif stages[name][0].valid:
                        stages[name][1]()

            pipeline(act, step)

        @block.vector
        def _(dve):
            def setup(name):
                ps = setup_ps[name]
                if name in SPLIT:
                    dve.wait_ge(setup_hi, SPLIT.index(name) + 1)
                    for a in range(C):
                        last = nc.vector.tensor_tensor(by_parts(name, w_lo[name][:, a, :]), by_heads(name, ps[:, a, :]),
                                                       by_parts(name, f32(w_hi[name][:, a, :])), ALU.subtract)
                    if name == "wo1":
                        last = nc.vector.tensor_copy(woT[:], ps[:])
                else:
                    dve.wait_ge(setup_ps_full, SETUP.index(name) + 1)
                    if name == "biases":
                        nc.vector.tensor_copy(g_bias[:], ps[:, 0, 0:C])
                        nc.vector.tensor_copy(key_const[:], ps[:, 0, C:C + 1])
                        last = nc.vector.tensor_copy(key_row[:], ps[:, 1, :])
                    else:
                        dve.wait_ge(layer1_landed, 16 * LAYER1_LOADS)
                        last = nc.vector.tensor_tensor(out_bias[:], ps[:, 0, :], bo1_row[:], ALU.add)
                last.then_inc(setup_copied, 1)

            def lo_part(lo, ps, hi):
                return nc.vector.tensor_tensor(lo, ps, f32(hi), ALU.subtract)

            def lo_biased(g, lo, ps, hi, bias, hi_done, lo_done):
                dve.wait_ge(hi_done, g.count(C))
                for a in range(C):
                    nc.vector.scalar_tensor_tensor(out=lo[:, a, :], in0=ps[:, a, :], scalar=bias[:, a:a + 1], in1=f32(hi[:, a, :]),
                                                   op0=ALU.add, op1=ALU.subtract).then_inc(lo_done, 1)

            def head_mask(g, h):
                dve.wait_ge(score_full, g.count(HEADS, h + 1))
                if h == 0:
                    dve.wait_ge(adjh_landed[g.parity], g.count_of_parity())
                before, hb = (g, h - RING) if h >= RING else (g + (-1), h + HEADS - RING)
                if before.started:
                    dve.wait_ge(probs_done, before.count(HEADS * C, (hb + 1) * C))
                dve.nop(nofuse=True)
                for c in range(C):
                    nc.vector.tensor_tensor_reduce(masked[h % RING][:, c, :], score_ps[h % 2][:, c, :], adj_heads[g.parity][:, c, :],
                                                   1.0, LOWEST, ALU.mult, ALU.max, row_max[:, h, c:c + 1]).then_inc(masked_done, 1)
                dve.wait_ge(masked_done, g.count(HEADS * C, (h + 1) * C))
                nc.vector.tensor_scalar(neg_max[:, h, :], row_max[:, h, :], -SCALE, None, ALU.mult).then_inc(neg_max_done, 1)

            def copy_pT(g, h):
                if h in ACT_PT:
                    return
                dve.wait_ge(pT_full, g.count(HEADS, h + 1))
                nc.vector.tensor_copy(pT_sb[h][:], pT_ps[h % 2][:]).then_inc(pT_by_dve, 1)

            def residual(g, h, ps, scale, plus, full, signal):
                dve.wait_ge(full, g.count())
                for c in range(C):
                    if scale is None:
                        nc.vector.tensor_tensor(h[:, c, :], ps[:, c, :], plus[:, c, :], ALU.add).then_inc(signal, 1)
                    else:
                        nc.vector.scalar_tensor_tensor(out=h[:, c, :], in0=ps[:, c, :], scalar=scale[:, c:c + 1], in1=plus[:, c, :],
                                                       op0=ALU.mult, op1=ALU.add).then_inc(signal, 1)

            def row_stats(i, g, h, signal):
                for c in range(C):
                    dve.wait_ge(signal, g.count(C, c + 1))
                    nc.vector.bn_stats(stats[i][:, c, :], h[:, c, :]).then_inc(stats_done[i], 1)
                for c in range(C):
                    dve.wait_ge(stats_done[i], g.count(C, c + 1))
                    dve.nop(nofuse=True)
                    nc.vector.bn_aggr(mean_var[i][:, c, :], stats[i][:, c, :]).then_inc(mean_var_done[i], 1)

            def step(t):
                coming, front, mid, tail = t + 3, t + 2, t + 1, t + (-1)

                def coming_xT():
                    dve.wait_ge(xT_hi_done, coming.count())
                    lo_part(xT_lo[:], xT_ps[:], xT_hi[:]).then_inc(xT_lo_done, 1)

                def tail_rsum():
                    dve.wait_ge(probs_done, tail.count(HEADS * C))
                    nc.vector.reciprocal(rsum[:], row_sum[tail.parity][:]).then_inc(rsum_done, 1)

                def front_g():
                    wait_setup(dve, front, "biases")
                    lo_biased(front, g_lo, g_ps, g_hi, g_bias, g_hi_done, g_lo_done)

                def front_rows():
                    dve.wait_ge(x_landed[front.parity], front.count_of_parity())
                    if (front + (-1)).started:
                        dve.wait_ge(row_bias_done, (front + (-1)).count())
                    for c in range(C):
                        nc.vector.tensor_tensor_reduce(scratch[:, c, :], x_sb[front.parity][:, c, :], key_row[:], 1.0, 0.0,
                                                       ALU.mult, ALU.add, row_dot[:, c:c + 1]).then_inc(row_dot_done, 1)
                    dve.wait_ge(row_dot_done, front.count(C))
                    if (front + (-1)).started:
                        dve.wait_ge(p0_done, (front + (-1)).count(C))
                    nc.vector.tensor_scalar(row_bias[:], row_dot[:], key_const[:, 0:1], None, ALU.add).then_inc(row_bias_done, 1)

                def mid_x1T():
                    dve.wait_ge(x1T_hi_done, mid.count())
                    lo_part(x1T_lo[:], x1T_ps[:], x1T_hi[:]).then_inc(x1T_lo_done, 1)

                def tail_oT():
                    dve.wait_ge(r_done, tail.count())
                    dve.wait_ge(oT_full, tail.count(GROUPS))
                    nc.vector.tensor_tensor(oT_sb[:], oT_ps[:], r_sb[:], ALU.mult).then_inc(oT_done, 1)

                def front_mask():
                    dve.wait_ge(adjf_landed[front.parity], front.count_of_parity())
                    for c in range(C):
                        dve.wait_ge(p0_done, front.count(C, c + 1))
                        nc.vector.tensor_tensor_reduce(p0m[:, c, :], p0[:, c, :], adj_front[front.parity][:, c, :], 1.0, 0.0,
                                                       ALU.mult, ALU.add, sum0[:, c:c + 1]).then_inc(p0m_done, 1)
                    dve.wait_ge(p0m_done, front.count(C))
                    nc.vector.reciprocal(rsum0[:], sum0[:]).then_inc(rsum0_done, 1)

                def mid_q():
                    if mid.peeled and mid.offset == 0:
                        dve.wait_ge(layer1_landed, 16 * LAYER1_LOADS)
                    lo_biased(mid, q_parts[:, 1], q_ps, q_parts[:, 0], bq1_col, q_hi_done, q_lo_done)

                def front_v0():
                    dve.wait_ge(v0_hi_done, front.count())
                    lo_part(v0_lo[:], v0_ps[:], v0_hi[:]).then_inc(v0_lo_done, 1)

                def front_p0T():
                    dve.wait_ge(p0T_hi_done, front.count())
                    lo_part(p0T_lo[:], p0T_ps[:], p0T_hi[:]).then_inc(p0T_lo_done, 1)

                def mid_k():
                    lo_biased(mid, k_parts[:, 1], k_ps, k_parts[:, 0], bk1_col, k_hi_done, k_lo_done)

                def tail_h1():
                    dve.wait_ge(x1_plus_done, tail.count())
                    if (tail + (-1)).started:
                        dve.wait_ge(out_done, (tail + (-1)).count())
                    residual(tail, h1, y_ps, None, x1_plus[tail.parity], y_full, h1_done)

                def tail_stats():
                    row_stats(1, tail, h1, h1_done)

                def front_h0():
                    dve.wait_ge(x_plus_done, front.count())
                    dve.wait_ge(rsum0_done, front.count())
                    if mid.started:
                        dve.wait_ge(x1_done, mid.count(C))
                    residual(front, h0, a0_ps, rsum0, x_plus, a0_full, h0_done)

                def mid_stats():
                    row_stats(0, mid, h0, h0_done)

                def mid_norm():
                    dve.wait_ge(rstd_done[0], mid.count())
                    if (mid + (-2)).started:
                        dve.wait_ge(x1_plus_done, (mid + (-2)).count())
                        dve.wait_ge(x1T_full, (mid + (-2)).count())
                    for c in range(C):
                        nc.vector.tensor_scalar(x1[mid.parity][:, c, :], h0[:, c, :], mean_var[0][:, c, 0:1], rstd[0][:, c:c + 1],
                                                ALU.subtract, ALU.mult).then_inc(x1_done, 1)

                stages = {"stats0": (mid, mid_stats), "rsum": (tail, tail_rsum), "norm0": (mid, mid_norm), "g": (front, front_g),
                          "x1T": (mid, mid_x1T), "rows": (front, front_rows), "q": (mid, mid_q), "oT": (tail, tail_oT),
                          "p0m": (front, front_mask), "k": (mid, mid_k), "h1": (tail, tail_h1), "stats1": (tail, tail_stats),
                          "v0": (front, front_v0), "p0T": (front, front_p0T), "xT": (coming, coming_xT), "h0": (front, front_h0)}
                for item in order_of(t, VECTOR_ORDER, VECTOR_FILL):
                    name, _, n = item.partition(":")
                    if name == "setup":
                        setup(n)
                    elif name == "mask":
                        if t.valid:
                            head_mask(t, int(n))
                    elif name == "copy":
                        g, h = lagging(t, int(n))
                        if g.valid:
                            copy_pT(g, h)
                    elif stages[name][0].valid:
                        stages[name][1]()

            pipeline(dve, step)


INPUTS = ["x", "adj", "L0_gnn_Wq_w", "L0_gnn_Wq_b", "L0_gnn_Wk_w", "L0_gnn_Wk_b", "L0_gnn_Wv_w", "L0_gnn_Wv_b",
          "L1_gnn_Wq", "L1_gnn_bq", "L1_gnn_Wk", "L1_gnn_bk", "L1_gnn_Wv", "L1_gnn_bv", "L1_gnn_Wo", "L1_gnn_bo"]


def kernel(**inputs):
    import numpy as np
    import concourse.bacc as bacc
    from concourse.bass_utils import run_bass_kernel_spmd

    nc = bacc.Bacc("TRN2", target_bir_lowering=False, num_devices=1)
    arrays, args = {}, []
    for name in INPUTS:
        a = np.ascontiguousarray(inputs[name])
        arrays[f"in_{name}"] = a
        args.append(nc.dram_tensor(f"in_{name}", a.shape, mybir.dt.from_np(a.dtype), kind="ExternalInput").ap())
    out = nc.dram_tensor("out_x", (B, N, D), F32, kind="ExternalOutput").ap()
    build(nc, *args, out)
    r = run_bass_kernel_spmd(nc, [arrays], core_ids=[0])
    return r.results[0]["out_x"]
```
